# Optimizing a Trainium2 kernel written in Bass

```python
import numpy as np
import jax
import jax.numpy as jnp

def _softmax(x, axis=-1):
    return jax.nn.softmax(x, axis=axis)

def _gelu(x):
    return jax.nn.gelu(x, approximate=True)

def _silu(x):
    return jax.nn.silu(x)

def _sigmoid(x):
    return jax.nn.sigmoid(x)

def _layernorm(x, axis=-1, eps=1e-05):
    m = jnp.mean(x, axis=axis, keepdims=True)
    v = jnp.var(x, axis=axis, keepdims=True)
    return (x - m) / jnp.sqrt(v + eps)

def _scatter_add(tgt, idx, src, axis=0):
    return tgt.at[idx].add(src)

def _segment_sum(src, seg, n):
    return jax.ops.segment_sum(src, seg, n)
kernel_name = 'mk_pixart_seq_d2_seqx_r4_3214d6'

def setup_inputs(seed: int=0):
    np.random.seed(seed)
    _w = jnp.asarray

    def _rec_inputs():
        import jax
        import jax.numpy as jnp
        _rk = jax.random.key(seed)
        x = -0.0002928 + 1 * jax.random.normal(jax.random.fold_in(_rk, 1), (32, 128, 256), jnp.float32)
        _lenS = 128 - jax.random.randint(jax.random.fold_in(_rk, 7), (32,), 0, max(1, 128 // 4) + 1, jnp.int32)
        _lenS2 = 128 - jax.random.randint(jax.random.fold_in(_rk, 8), (32,), 0, max(1, 128 // 4) + 1, jnp.int32)
        cond_1024 = 0.0061147 + 1.02565 * jax.random.normal(jax.random.fold_in(_rk, 11), (32, 256), jnp.float32)
        _ctx_1024P = jax.random.normal(jax.random.fold_in(_rk, 12), (32, 16, 256), jnp.float32)
        _ctx_1024c = jax.random.dirichlet(jax.random.fold_in(_rk, 512), 0.3 * jnp.ones((16,), jnp.float32), (32, 128))
        _ctx_1024t = jnp.einsum('bsk,bkd->bsd', _ctx_1024c, _ctx_1024P)
        _ctx_1024t = _ctx_1024t * jax.lax.rsqrt(jnp.mean(jnp.square(_ctx_1024t)) + 1e-12) * 0.953939
        ctx_1024 = -0.00265004 + 0.998804 * (_ctx_1024t + 0.3 * jax.random.normal(jax.random.fold_in(_rk, 612), (32, 128, 256), jnp.float32))
        _validS = jnp.arange(128)[None, :] < _lenS[:, None]
        _validS2 = jnp.arange(128)[None, :] < _lenS2[:, None]
        _causal = jnp.tril(jnp.ones((128, 128), dtype=bool))
        mask_BxS2_bf0 = jnp.logical_not(jnp.ones((32, 128), dtype=bool))
        return (x, cond_1024, ctx_1024, mask_BxS2_bf0)
    x, cond_1024, ctx_1024, mask_BxS2_bf0 = _rec_inputs()

    def _L0_xcond_setup():
        import jax, jax.numpy as jnp
        import numpy as np
        D, H, B, N, S = (256, 16, 4, 256, 77)
        HD = D // H
        DF = 4 * D
        EPS = 1e-06
        SCALE = HD ** (-0.5)

        def _ln(x):
            m = jnp.mean(x, axis=-1, keepdims=True)
            v = jnp.mean((x - m) ** 2, axis=-1, keepdims=True)
            return (x - m) / jnp.sqrt(v + EPS)
        key = jax.random.key(seed)
        ks = jax.random.split(key, 24)
        s = 0.02
        inp = {'x': jax.random.normal(ks[0], (B, N, D), jnp.float32), 't_emb': jax.random.normal(ks[1], (B, D), jnp.float32), 'context': jax.random.normal(ks[2], (B, S, D), jnp.float32), 'context_mask': jnp.zeros((B, S), jnp.bool_), 'ada_w': jax.random.normal(ks[3], (D, 6 * D), jnp.float32) * s, 'ada_b': jnp.zeros((6 * D,), jnp.float32), 'qkv_w': jax.random.normal(ks[4], (D, 3 * D), jnp.float32) * s, 'qkv_b': jnp.zeros((3 * D,), jnp.float32), 'sa_proj_w': jax.random.normal(ks[5], (D, D), jnp.float32) * s, 'sa_proj_b': jnp.zeros((D,), jnp.float32), 'q_w': jax.random.normal(ks[6], (D, D), jnp.float32) * s, 'q_b': jnp.zeros((D,), jnp.float32), 'kv_w': jax.random.normal(ks[7], (D, 2 * D), jnp.float32) * s, 'kv_b': jnp.zeros((2 * D,), jnp.float32), 'ca_proj_w': jax.random.normal(ks[8], (D, D), jnp.float32) * s, 'ca_proj_b': jnp.zeros((D,), jnp.float32), 'fc1_w': jax.random.normal(ks[9], (D, DF), jnp.float32) * s, 'fc1_b': jnp.zeros((DF,), jnp.float32), 'fc2_w': jax.random.normal(ks[10], (DF, D), jnp.float32) * s, 'fc2_b': jnp.zeros((D,), jnp.float32)}
        return inp
    _L0_xcond_all = _L0_xcond_setup()
    _L0_xcond_in = {k: v for k, v in _L0_xcond_all.items() if k in ('ada_w', 'ada_b', 'qkv_w', 'qkv_b', 'sa_proj_w', 'sa_proj_b', 'q_w', 'q_b', 'kv_w', 'kv_b', 'ca_proj_w', 'ca_proj_b', 'fc1_w', 'fc1_b', 'fc2_w', 'fc2_b')}
    del _L0_xcond_all

    def _L1_xcond_setup():
        import jax, jax.numpy as jnp
        import numpy as np
        import math
        D_MODEL = 256
        N_HEADS = 16
        HEAD_DIM = D_MODEL // N_HEADS
        D_FF = 1024
        EPS = 1e-05
        ROPE_BASE = 10000.0

        def _rope(t):
            L, Dh = (t.shape[1], t.shape[-1])
            half = Dh // 2
            inv_freq = 1.0 / ROPE_BASE ** (jnp.arange(half, dtype=t.dtype) / half)
            ang = jnp.arange(L, dtype=t.dtype)[:, None] * inv_freq[None, :]
            cos = jnp.cos(ang)[None, :, None, :]
            sin = jnp.sin(ang)[None, :, None, :]
            t1, t2 = (t[..., :half], t[..., half:])
            return jnp.concatenate([t1 * cos - t2 * sin, t2 * cos + t1 * sin], axis=-1)

        def _adaln(x, emb, w, b):
            e = emb[:, 0, :]
            gb = e @ w.T + b
            gamma, beta = jnp.split(gb, 2, axis=-1)
            mu = x.mean(-1, keepdims=True)
            var = x.var(-1, keepdims=True)
            xn = (x - mu) * jax.lax.rsqrt(var + EPS)
            return xn * (1.0 + gamma[:, None, :]) + beta[:, None, :]

        def _attn(q, k, v):
            scale = 1.0 / math.sqrt(HEAD_DIM)
            scores = jnp.einsum('bqhd,bkhd->bhqk', q, k) * scale
            w = jax.nn.softmax(scores, axis=-1)
            out = jnp.einsum('bhqk,bkhd->bqhd', w, v)
            B, Lq = (out.shape[0], out.shape[1])
            return out.reshape(B, Lq, D_MODEL)
        key = jax.random.key(seed)
        ks = jax.random.split(key, 24)
        s = 0.02
        inp = {'x': jax.random.normal(ks[0], (2, 512, D_MODEL), jnp.float32), 'noise_emb': jax.random.normal(ks[1], (2, 1, D_MODEL), jnp.float32), 'context': jax.random.normal(ks[2], (2, 256, D_MODEL), jnp.float32), 'ln1_w': jax.random.normal(ks[3], (2 * D_MODEL, D_MODEL), jnp.float32) * s, 'ln1_b': jax.random.normal(ks[4], (2 * D_MODEL,), jnp.float32) * s, 'ln2_w': jax.random.normal(ks[5], (2 * D_MODEL, D_MODEL), jnp.float32) * s, 'ln2_b': jax.random.normal(ks[6], (2 * D_MODEL,), jnp.float32) * s, 'ln3_w': jax.random.normal(ks[7], (2 * D_MODEL, D_MODEL), jnp.float32) * s, 'ln3_b': jax.random.normal(ks[8], (2 * D_MODEL,), jnp.float32) * s, 'qkv_w': jax.random.normal(ks[9], (3 * D_MODEL, D_MODEL), jnp.float32) * s, 'sa_out_w': jax.random.normal(ks[10], (D_MODEL, D_MODEL), jnp.float32) * s, 'q_w': jax.random.normal(ks[11], (D_MODEL, D_MODEL), jnp.float32) * s, 'k_w': jax.random.normal(ks[12], (D_MODEL, D_MODEL), jnp.float32) * s, 'v_w': jax.random.normal(ks[13], (D_MODEL, D_MODEL), jnp.float32) * s, 'ca_out_w': jax.random.normal(ks[14], (D_MODEL, D_MODEL), jnp.float32) * s, 'ffn_w1': jax.random.normal(ks[15], (D_FF, D_MODEL), jnp.float32) * s, 'ffn_b1': jax.random.normal(ks[16], (D_FF,), jnp.float32) * s, 'ffn_w2': jax.random.normal(ks[17], (D_MODEL, D_FF), jnp.float32) * s, 'ffn_b2': jax.random.normal(ks[18], (D_MODEL,), jnp.float32) * s}
        return inp
    _L1_xcond_all = _L1_xcond_setup()
    _L1_xcond_in = {k: v for k, v in _L1_xcond_all.items() if k in ('ln1_w', 'ln1_b', 'ln2_w', 'ln2_b', 'ln3_w', 'ln3_b', 'qkv_w', 'sa_out_w', 'q_w', 'k_w', 'v_w', 'ca_out_w', 'ffn_w1', 'ffn_b1', 'ffn_w2', 'ffn_b2')}
    del _L1_xcond_all
    return {'x': x, 'cond_1024': cond_1024, 'ctx_1024': ctx_1024, 'mask_BxS2_bf0': mask_BxS2_bf0, 'L0_xcond_ada_w': _L0_xcond_in['ada_w'], 'L0_xcond_ada_b': _L0_xcond_in['ada_b'], 'L0_xcond_qkv_w': _L0_xcond_in['qkv_w'], 'L0_xcond_qkv_b': _L0_xcond_in['qkv_b'], 'L0_xcond_sa_proj_w': _L0_xcond_in['sa_proj_w'], 'L0_xcond_sa_proj_b': _L0_xcond_in['sa_proj_b'], 'L0_xcond_q_w': _L0_xcond_in['q_w'], 'L0_xcond_q_b': _L0_xcond_in['q_b'], 'L0_xcond_kv_w': _L0_xcond_in['kv_w'], 'L0_xcond_kv_b': _L0_xcond_in['kv_b'], 'L0_xcond_ca_proj_w': _L0_xcond_in['ca_proj_w'], 'L0_xcond_ca_proj_b': _L0_xcond_in['ca_proj_b'], 'L0_xcond_fc1_w': _L0_xcond_in['fc1_w'], 'L0_xcond_fc1_b': _L0_xcond_in['fc1_b'], 'L0_xcond_fc2_w': _L0_xcond_in['fc2_w'], 'L0_xcond_fc2_b': _L0_xcond_in['fc2_b'], 'L1_xcond_ln1_w': _L1_xcond_in['ln1_w'], 'L1_xcond_ln1_b': _L1_xcond_in['ln1_b'], 'L1_xcond_ln2_w': _L1_xcond_in['ln2_w'], 'L1_xcond_ln2_b': _L1_xcond_in['ln2_b'], 'L1_xcond_ln3_w': _L1_xcond_in['ln3_w'], 'L1_xcond_ln3_b': _L1_xcond_in['ln3_b'], 'L1_xcond_qkv_w': _L1_xcond_in['qkv_w'], 'L1_xcond_sa_out_w': _L1_xcond_in['sa_out_w'], 'L1_xcond_q_w': _L1_xcond_in['q_w'], 'L1_xcond_k_w': _L1_xcond_in['k_w'], 'L1_xcond_v_w': _L1_xcond_in['v_w'], 'L1_xcond_ca_out_w': _L1_xcond_in['ca_out_w'], 'L1_xcond_ffn_w1': _L1_xcond_in['ffn_w1'], 'L1_xcond_ffn_b1': _L1_xcond_in['ffn_b1'], 'L1_xcond_ffn_w2': _L1_xcond_in['ffn_w2'], 'L1_xcond_ffn_b2': _L1_xcond_in['ffn_b2']}

def reference(x, cond_1024, ctx_1024, mask_BxS2_bf0, L0_xcond_ada_w, L0_xcond_ada_b, L0_xcond_qkv_w, L0_xcond_qkv_b, L0_xcond_sa_proj_w, L0_xcond_sa_proj_b, L0_xcond_q_w, L0_xcond_q_b, L0_xcond_kv_w, L0_xcond_kv_b, L0_xcond_ca_proj_w, L0_xcond_ca_proj_b, L0_xcond_fc1_w, L0_xcond_fc1_b, L0_xcond_fc2_w, L0_xcond_fc2_b, L1_xcond_ln1_w, L1_xcond_ln1_b, L1_xcond_ln2_w, L1_xcond_ln2_b, L1_xcond_ln3_w, L1_xcond_ln3_b, L1_xcond_qkv_w, L1_xcond_sa_out_w, L1_xcond_q_w, L1_xcond_k_w, L1_xcond_v_w, L1_xcond_ca_out_w, L1_xcond_ffn_w1, L1_xcond_ffn_b1, L1_xcond_ffn_w2, L1_xcond_ffn_b2):
    import jax
    import jax.numpy as jnp

    def _L0_xcond_ref(x, t_emb, context, context_mask, ada_w, ada_b, qkv_w, qkv_b, sa_proj_w, sa_proj_b, q_w, q_b, kv_w, kv_b, ca_proj_w, ca_proj_b, fc1_w, fc1_b, fc2_w, fc2_b):
        import jax, jax.numpy as jnp
        import numpy as np
        D, H, B, N, S = (256, 16, 4, 256, 77)
        HD = D // H
        DF = 4 * D
        EPS = 1e-06
        SCALE = HD ** (-0.5)

        def _ln(x):
            m = jnp.mean(x, axis=-1, keepdims=True)
            v = jnp.mean((x - m) ** 2, axis=-1, keepdims=True)
            return (x - m) / jnp.sqrt(v + EPS)
        Bx, Nx, C = x.shape
        Sx = context.shape[1]
        mod = jax.nn.silu(t_emb) @ ada_w + ada_b
        shift_sa, scale_sa, gate_sa, shift_ff, scale_ff, gate_ff = [m[:, None, :] for m in jnp.split(mod, 6, axis=-1)]
        xm1 = _ln(x) * (1 + scale_sa) + shift_sa
        qkv = (xm1 @ qkv_w + qkv_b).reshape(Bx, Nx, 3, H, HD)
        q, k, v = (qkv[:, :, 0], qkv[:, :, 1], qkv[:, :, 2])
        attn = jnp.einsum('bnhd,bmhd->bhnm', q, k) * SCALE
        attn = jax.nn.softmax(attn, axis=-1)
        sa = jnp.einsum('bhnm,bmhd->bnhd', attn, v).reshape(Bx, Nx, C)
        sa = sa @ sa_proj_w + sa_proj_b
        x = x + gate_sa * sa
        xn2 = _ln(x)
        qc = (xn2 @ q_w + q_b).reshape(Bx, Nx, H, HD)
        kvc = (context @ kv_w + kv_b).reshape(Bx, Sx, 2, H, HD)
        kc, vc = (kvc[:, :, 0], kvc[:, :, 1])
        attn_c = jnp.einsum('bnhd,bshd->bhns', qc, kc) * SCALE
        attn_c = jnp.where(context_mask[:, None, None, :], -jnp.inf, attn_c)
        attn_c = jax.nn.softmax(attn_c, axis=-1)
        ca = jnp.einsum('bhns,bshd->bnhd', attn_c, vc).reshape(Bx, Nx, C)
        ca = ca @ ca_proj_w + ca_proj_b
        x = x + ca
        xm3 = _ln(x) * (1 + scale_ff) + shift_ff
        h = jax.nn.gelu(xm3 @ fc1_w + fc1_b, approximate=False)
        ff = h @ fc2_w + fc2_b
        x = x + gate_ff * ff
        return x

    def _L1_xcond_ref(x, noise_emb, context, ln1_w, ln1_b, ln2_w, ln2_b, ln3_w, ln3_b, qkv_w, sa_out_w, q_w, k_w, v_w, ca_out_w, ffn_w1, ffn_b1, ffn_w2, ffn_b2):
        import jax, jax.numpy as jnp
        import numpy as np
        import math
        D_MODEL = 256
        N_HEADS = 16
        HEAD_DIM = D_MODEL // N_HEADS
        D_FF = 1024
        EPS = 1e-05
        ROPE_BASE = 10000.0

        def _rope(t):
            L, Dh = (t.shape[1], t.shape[-1])
            half = Dh // 2
            inv_freq = 1.0 / ROPE_BASE ** (jnp.arange(half, dtype=t.dtype) / half)
            ang = jnp.arange(L, dtype=t.dtype)[:, None] * inv_freq[None, :]
            cos = jnp.cos(ang)[None, :, None, :]
            sin = jnp.sin(ang)[None, :, None, :]
            t1, t2 = (t[..., :half], t[..., half:])
            return jnp.concatenate([t1 * cos - t2 * sin, t2 * cos + t1 * sin], axis=-1)

        def _adaln(x, emb, w, b):
            e = emb[:, 0, :]
            gb = e @ w.T + b
            gamma, beta = jnp.split(gb, 2, axis=-1)
            mu = x.mean(-1, keepdims=True)
            var = x.var(-1, keepdims=True)
            xn = (x - mu) * jax.lax.rsqrt(var + EPS)
            return xn * (1.0 + gamma[:, None, :]) + beta[:, None, :]

        def _attn(q, k, v):
            scale = 1.0 / math.sqrt(HEAD_DIM)
            scores = jnp.einsum('bqhd,bkhd->bhqk', q, k) * scale
            w = jax.nn.softmax(scores, axis=-1)
            out = jnp.einsum('bhqk,bkhd->bqhd', w, v)
            B, Lq = (out.shape[0], out.shape[1])
            return out.reshape(B, Lq, D_MODEL)
        B, L, D = x.shape
        L_ctx = context.shape[1]
        res = x
        xn = _adaln(x, noise_emb, ln1_w, ln1_b)
        qkv = xn @ qkv_w.T
        q, k, v = jnp.split(qkv, 3, axis=-1)
        q = _rope(q.reshape(B, L, N_HEADS, HEAD_DIM))
        k = _rope(k.reshape(B, L, N_HEADS, HEAD_DIM))
        v = v.reshape(B, L, N_HEADS, HEAD_DIM)
        sa = _attn(q, k, v) @ sa_out_w.T
        x = res + sa
        res = x
        xn = _adaln(x, noise_emb, ln2_w, ln2_b)
        q = _rope((xn @ q_w.T).reshape(B, L, N_HEADS, HEAD_DIM))
        k = _rope((context @ k_w.T).reshape(B, L_ctx, N_HEADS, HEAD_DIM))
        v = (context @ v_w.T).reshape(B, L_ctx, N_HEADS, HEAD_DIM)
        ca = _attn(q, k, v) @ ca_out_w.T
        x = res + ca
        res = x
        xn = _adaln(x, noise_emb, ln3_w, ln3_b)
        h = jax.nn.gelu(xn @ ffn_w1.T + ffn_b1, approximate=False)
        x = res + (h @ ffn_w2.T + ffn_b2)
        return x
    x = _L0_xcond_ref(x, cond_1024, ctx_1024, mask_BxS2_bf0, L0_xcond_ada_w, L0_xcond_ada_b, L0_xcond_qkv_w, L0_xcond_qkv_b, L0_xcond_sa_proj_w, L0_xcond_sa_proj_b, L0_xcond_q_w, L0_xcond_q_b, L0_xcond_kv_w, L0_xcond_kv_b, L0_xcond_ca_proj_w, L0_xcond_ca_proj_b, L0_xcond_fc1_w, L0_xcond_fc1_b, L0_xcond_fc2_w, L0_xcond_fc2_b)
    x = _L1_xcond_ref(x, cond_1024[:, None, :], ctx_1024, L1_xcond_ln1_w, L1_xcond_ln1_b, L1_xcond_ln2_w, L1_xcond_ln2_b, L1_xcond_ln3_w, L1_xcond_ln3_b, L1_xcond_qkv_w, L1_xcond_sa_out_w, L1_xcond_q_w, L1_xcond_k_w, L1_xcond_v_w, L1_xcond_ca_out_w, L1_xcond_ffn_w1, L1_xcond_ffn_b1, L1_xcond_ffn_w2, L1_xcond_ffn_b2)
    return x

_drawn_inputs = setup_inputs


def setup_inputs(seed=0):
    import zlib

    import numpy as np

    out = dict(_drawn_inputs(seed))
    spreads = {'L0_xcond_ada_b': (0.0, 0.384),
     'L0_xcond_qkv_b': (0.0, 0.8),
     'L0_xcond_sa_proj_b': (0.0, 0.338),
     'L0_xcond_q_b': (0.0, 2.0),
     'L0_xcond_kv_b': (0.0, 0.618),
     'L0_xcond_ca_proj_b': (0.0, 0.1),
     'L0_xcond_fc1_b': (0.0, 0.8),
     'L0_xcond_fc2_b': (0.0, 0.379)}
    factors = {'L0_xcond_qkv_w': 8.0,
     'L0_xcond_sa_proj_w': 6.308,
     'L0_xcond_q_w': 64.0,
     'L1_xcond_ln1_b': 64.0,
     'L1_xcond_ln2_w': 8.0,
     'L1_xcond_ln2_b': 49.499,
     'L1_xcond_ln3_b': 45.887,
     'L1_xcond_q_w': 8.0,
     'L1_xcond_k_w': 8.0,
     'L1_xcond_ffn_b1': 7.629,
     'L1_xcond_ffn_b2': 2.91,
     'L1_xcond_ln1_w': 3.935,
     'L1_xcond_ln3_w': 2.768}
    for name, (base, spread) in spreads.items():
        noise = np.random.default_rng([zlib.crc32(name.encode()), seed]).standard_normal(out[name].shape)
        drawn = base * np.exp(spread * noise) if base else spread * noise
        out[name] = jnp.asarray(drawn.astype(out[name].dtype))
    for name, factor in factors.items():
        out[name] = (out[name] * factor).astype(out[name].dtype)
    return out
```

```python
from contextlib import ExitStack

import numpy as np
import concourse.bass as bass
from concourse import mybir

F32 = mybir.dt.float32
F32R = mybir.dt.float32r
BF16 = mybir.dt.bfloat16
U8 = mybir.dt.uint8
U32 = mybir.dt.uint32
ALU = mybir.AluOpType
ACT = mybir.ActivationFunctionType
AX = mybir.AxisListType

P = 128
B, N, D, H = 32, 128, 256, 16
HD = D // H
DF = 4 * D
CT = D // P
FT = DF // P
GB = 4
NG = B // GB
GN = GB * N
LAYERS = 2
EPS = (1e-6, 1e-5)
SCALE = HD ** -0.5
MASKED = -1e30
QUADS = 4
STEPS = GB * QUADS
SELF, CROSS = 0, 1

W_QKV = 0
W_SA = W_QKV + CT * 3 * D
W_Q = W_SA + CT * D
W_KV = W_Q + CT * D
W_CA = W_KV + CT * 2 * D
W_F1 = W_CA + CT * D
W_F2 = W_F1 + CT * DF
W_ALL = W_F2 + FT * D
CHUNK = W_ALL // 4

SELF_TILES = [("k", 0), ("k", 1), ("q", 0), ("q", 1)] + [("v", b) for b in range(GB)]
CROSS_TILES = [("k", 0), ("k", 1)] + [("v", b) for b in range(GB)] + [("q", 0), ("q", 1)]
TILES = ([(SELF, *t) for t in SELF_TILES] + [(CROSS, *t) for t in CROSS_TILES]
         + [(None, "f", f) for f in range(FT)])
RING = 4
PER_BANK = len(TILES) // RING
HID_SLOTS = 4

AT_TURN = 2
AT_RDEN, AT_MIX, AT_SCALE, AT_PROJ, AT_STATS, AT_Z, AT_LNT = 5, 6, 7, 8, 9, 10, 11
LAST_STEP = QUADS * (GB - 1) + AT_LNT


def tile_of(s, kind, i):
    return TILES.index((s, kind, i))


def batch_at(step, lag):
    b, r = divmod(step - lag, QUADS)
    return b if r == 0 and 0 <= b < GB else None


def build_blocks(nc, a, x_mid, gates_dram, out):
    ctx = ExitStack()
    with ctx:
        def sb(name, shape, dt=F32):
            return ctx.enter_context(nc.sbuf_tensor(name, shape, dt))

        def bank(name):
            return ctx.enter_context(nc.psum_tensor(name, [P, 512], F32))

        def sem(name):
            return ctx.enter_context(nc.semaphore(name))

        w_hi = sb("w_hi", [P, W_ALL], F32R)
        w_lo = sb("w_lo", [P, W_ALL], F32R)
        ident = sb("ident", [P, P])
        head_mask = sb("head_mask", [P, 2])
        cos_t = sb("cos_t", [P, N])
        sin_t = sb("sin_t", [P, N])
        ones_row = sb("ones_row", [P, P], BF16)
        minus_half = sb("minus_half", [P, 1])
        bias_rows = sb("bias_rows", [P, 6, D])
        bias_cols = sb("bias_cols", [P, 8 + 2 * FT])
        bias_mod = sb("bias_mod", [P, 20])
        mod = sb("mod", [P, LAYERS, 3, CT, 2, B])
        mod_now = sb("mod_now", [P, 3 * CT * 2, GB])
        cond = sb("cond", [P, CT, B])
        silu = sb("silu", [P, CT, B])
        silu_tmp = sb("silu_tmp", [P, CT, B])
        gate_bias = sb("gate_bias", [B, 2, D])
        gate_rows = sb("gate_rows", [B, 2, D])
        gate_now = sb("gate_now", [P, GB, 2, D])
        mask_u8 = sb("mask_u8", [P, GN], U8)
        mask_row = sb("mask_row", [P, GN], BF16)
        x_new = sb("x_new", [P, GB, D])
        x = sb("x", [P, GB, D])
        stats = sb("stats", [P, GB, 6])
        mean_var = sb("mean_var", [P, GB, 2])
        var_eps = sb("var_eps", [P, GB])
        rstd = sb("rstd", [P, GB])
        z = sb("z", [P, GB, D])
        xt = sb("xt", [P, 2, CT, N])
        xt_hi = sb("xt_hi", [P, CT, GN], F32R)
        xt_lo = sb("xt_lo", [P, CT, GN], F32R)
        ctxt = sb("ctxt", [P, CT, GN])
        ctx_hi = sb("ctx_hi", [P, CT, GN], F32R)
        ctx_lo = sb("ctx_lo", [P, CT, GN], F32R)
        q_t = sb("q_t", [P, CT, GN])
        k_t = sb("k_t", [P, CT, 2, GN])
        v_pad = sb("v_pad", [P, GB, H, 2 * HD])
        raw = sb("raw", [P, 2, GN])
        rot = sb("rot", [P, GN])
        straight = sb("straight", [P, 2, GN])
        neg_max = sb("neg_max", [P, 2, 4])
        probs = sb("probs", [P, 3, 4, N])
        row_sum = sb("row_sum", [P, 2, H])
        rden = sb("rden", [P, 2, H])
        rden_wide = sb("rden_wide", [P, D])
        rden_t = sb("rden_t", [P, D])
        probs_t = sb("probs_t", [P, 2, QUADS, 4, N])
        heads = sb("heads", [P, 2, CT, N])
        heads_hi = sb("heads_hi", [P, 2, CT, N], F32R)
        heads_lo = sb("heads_lo", [P, 2, CT, N], F32R)
        delta = sb("delta", [P, 2, D])
        hid = raw
        hid_hi = sb("hid_hi", [P, HID_SLOTS, GN], F32R)
        hid_lo = sb("hid_lo", [P, HID_SLOTS, GN], F32R)
        stage = probs_t[:, :, :, :, :].rearrange("p a q s n -> p (a q s n)")

        ring = [bank(f"ring{r}") for r in range(RING)]
        mix = [bank(f"mix{r}") for r in range(2)]
        p_proj = bank("p_proj")
        p_ln = bank("p_ln")
        y_mlp = [mix[0], mix[1], p_proj, p_ln]

        c_loaded = sem("c_loaded")
        ready = sem("ready")
        dve_held = sem("dve_held")
        pool_held = sem("pool_held")
        half_made = sem("half_made")
        silu_step = sem("silu_step")
        mod_full = sem("mod_full")
        mod_step = sem("mod_step")
        gates_made = sem("gates_made")
        w_loaded = [sem(f"w_loaded{h}") for h in range(2)]
        w_hi_made = sem("w_hi_made")
        w_lo_made = sem("w_lo_made")
        stored = sem("stored")
        x_loaded = sem("x_loaded")
        ctx_loaded = sem("ctx_loaded")
        side_loaded = sem("side_loaded")
        mask_made = sem("mask_made")
        mod_copied = sem("mod_copied")
        ctx_hi_made = sem("ctx_hi_made")
        ctx_lo_made = sem("ctx_lo_made")
        stats_made = sem("stats_made")
        moments_made = sem("moments_made")
        eps_added = sem("eps_added")
        rstd_made = sem("rstd_made")
        z_made = sem("z_made")
        z_turned = sem("z_turned")
        ln_moved = sem("ln_moved")
        xt_hi_made = sem("xt_hi_made")
        xt_lo_made = sem("xt_lo_made")
        tile_full = sem("tile_full")
        moved = [sem(f"moved{r}") for r in range(RING)]
        shuffled = sem("shuffled")
        cos_made = sem("cos_made")
        rot_step = sem("rot_step")
        keys_made = sem("keys_made")
        queries_made = sem("queries_made")
        scored = sem("scored")
        max_made = sem("max_made")
        exps_made = sem("exps_made")
        probs_turned = sem("probs_turned")
        probs_moved = sem("probs_moved")
        rden_made = sem("rden_made")
        rden_spread = sem("rden_spread")
        mixed = sem("mixed")
        rden_turned = sem("rden_turned")
        rden_moved = sem("rden_moved")
        heads_scaled = sem("heads_scaled")
        heads_hi_made = sem("heads_hi_made")
        heads_lo_made = sem("heads_lo_made")
        projected = sem("projected")
        hid_used = sem("hid_used")
        fc2_full = sem("fc2_full")
        y_moved = sem("y_moved")
        gated = sem("gated")
        x_updated = sem("x_updated")
        hid_hi_made = sem("hid_hi_made")
        hid_lo_made = sem("hid_lo_made")

        GATE_STORES = 1
        CONST_LOADS = 13

        def moved_by(eng, it, n):
            eng.wait_ge(moved[n % RING], it * PER_BANK + n // RING + 1)

        def x_ready(eng, layer, g, j):
            if layer == 0:
                eng.wait_ge(x_updated, g * 12 + j + 1)
            elif j < 8:
                eng.wait_ge(y_moved, (g + NG) * 12 + j + 1)
            else:
                eng.wait_ge(x_updated, g * 4 + 12 * NG + j - 8 + 1)

        block = ctx.enter_context(nc.Block())

        @block.sync
        def _(sp):
            for dst, src in (
                (cond[:], a["condT"].rearrange("(t p) b -> p t b", p=P)),
                (stage[:, 0:CT * 6 * D].rearrange("p (t n) -> p t n", t=CT),
                 a["L0_xcond_ada_w"].rearrange("(t p) n -> p t n", p=P)),
                (k_t[:].rearrange("p t e n -> p (t e n)").rearrange("p (m t n) -> p m t n", m=2, t=CT),
                 a["ln_wT"][0:2].rearrange("m (t p) n -> p m t n", p=P)),
                (q_t[:], a["ln_wT"][2].rearrange("(t p) n -> p t n", p=P)),
                (bias_mod[:], a["bias_mod"]),
                (gate_bias[:], a["gate_bias"].partition_broadcast(B)),
                (ident[:], a["ident"]),
                (head_mask[:], a["head_mask"]),
                (cos_t[:], a["cos_t"]),
                (sin_t[:], a["sin_t"]),
                (bias_rows[:], a["bias_rows"].partition_broadcast(P)),
                (bias_cols[:], a["bias_cols"]),
            ):
                sp.dma_start(dst, src).then_inc(c_loaded, 16)
            sp.dma_start(ctxt[:], a["ctxT"][:, 0:GN].rearrange("(t p) n -> p t n", p=P)).then_inc(ctx_loaded, 16)
            sp.dma_start(x_new[:], a["x"][0:GN, :].rearrange("(b p) c -> p b c", p=P)).then_inc(x_loaded, 16)

            def load_weights(layer):
                for c, parts in enumerate(WEIGHTS[layer]):
                    n = 4 * layer + c
                    if n >= 2 and c >= 2:
                        sp.wait_ge(w_hi_made, n - 1)
                        sp.wait_ge(w_lo_made, n - 1)
                    for name, col, kt, width in parts:
                        at = col - c * CHUNK + (c % 2) * CHUNK
                        dst = stage[:, at:at + kt * width].rearrange("p (t n) -> p t n", t=kt)
                        sp.dma_start(dst, a[name].rearrange("(t p) n -> p t n", p=P)).then_inc(w_loaded[c % 2], 16)

            sp.wait_ge(mod_full, 2)
            load_weights(0)
            sp.wait_ge(gates_made, 1)
            sp.dma_start(gates_dram, gate_rows[:]).then_inc(stored, 16)
            sp.wait_ge(stored, 16)

            def side(i):
                sp.dma_start(gate_now[:].rearrange("p b g c -> p (b g c)"),
                             gates_dram[bass.ds(i * GB, GB)].rearrange("b g c -> (b g c)")
                             .partition_broadcast(P)).then_inc(side_loaded, 16)
                sp.dma_start(mask_u8[:].bitcast(U32), a["mask"][bass.ds(i * (GN // 4), GN // 4)].partition_broadcast(P)).then_inc(side_loaded, 16)

            def load_ctx(i):
                sp.dma_start(ctxt[:], a["ctxT"][:, bass.ds(i * GN, GN)].rearrange("(t p) n -> p t n", p=P))\
                  .then_inc(ctx_loaded, 16)

            def load_x(src, i):
                sp.dma_start(x_new[:], src[bass.ds(i * GN, GN), :].rearrange("(b p) c -> p b c", p=P))\
                  .then_inc(x_loaded, 16)

            def store_x(dst, layer, i):
                x_ready(sp, layer, i, 11)
                sp.dma_start(dst[bass.ds(i * GN, GN), :].rearrange("(b p) c -> p b c", p=P), x[:]).then_inc(stored, 16)

            side(0)
            with sp.Fori(0, NG - 1) as i:
                sp.wait_ge(ctx_lo_made, i + 1)
                load_ctx(i + 1)
                x_ready(sp, 0, i, 3)
                load_x(a["x"], i + 1)
                x_ready(sp, 0, i, 11)
                side(i + 1)
                store_x(x_mid, 0, i)
            sp.wait_ge(ctx_lo_made, NG)
            load_ctx(0)
            sp.wait_ge(tile_full, (NG - 1) * len(TILES) + tile_of(None, "f", 0) + 1)
            x_ready(sp, 0, NG - 1, 11)
            store_x(x_mid, 0, NG - 1)
            sp.wait_ge(stored, 16 * (GATE_STORES + NG))
            load_x(x_mid, 0)
            load_weights(1)
            with sp.Fori(0, NG - 1) as i:
                sp.wait_ge(ctx_lo_made, i + NG + 1)
                load_ctx(i + 1)
                x_ready(sp, 1, i, 3)
                load_x(x_mid, i + 1)
                store_x(out, 1, i)
            store_x(out, 1, NG - 1)
            sp.wait_ge(stored, 16 * (GATE_STORES + LAYERS * NG))

        @block.tensor
        def _(pe):
            def product(dst, lhs, rhs, first, last):
                pe.matmul(dst, lhs[1], rhs[0], start=first, stop=False)
                pe.matmul(dst, lhs[0], rhs[1], start=False, stop=False)
                return pe.matmul(dst, lhs[0], rhs[0], start=False, stop=last)

            def w(col, kt, stride, lo, width):
                c = col + kt * stride + lo
                return w_hi[:, c:c + width], w_lo[:, c:c + width]

            def turn_z(it, k, b):
                pe.wait_ge(z_made, it * 12 + 4 * k + b + 1)
                if 4 * k + b:
                    pe.wait_ge(ln_moved, it * 12 + 4 * k + b)
                for c in range(CT):
                    mm = pe.transpose(p_ln[:, c * P:(c + 1) * P], z[:, b, c * P:(c + 1) * P], ident[:])
                mm.then_inc(z_turned, 1)

            def big_tile(it, n):
                s, kind, i = TILES[n]
                if n % 8 >= RING:
                    moved_by(pe, it, n - RING)
                src = (ctx_hi, ctx_lo) if s == CROSS and kind != "q" else (xt_hi, xt_lo)
                if n in (8,):
                    pe.wait_ge(ctx_hi_made, it + 1)
                    pe.wait_ge(ctx_lo_made, it + 1)
                if n in (0, 14, 16):
                    k = {0: 0, 14: 1, 16: 2}[n]
                    pe.wait_ge(xt_hi_made, it * 12 + 4 * k + 4)
                    pe.wait_ge(xt_lo_made, it * 12 + 4 * k + 4)
                dst = ring[n % RING]
                for c in range(CT):
                    act = tuple(t[:, c, :] for t in src)
                    if kind == "v":
                        act = tuple(t[:, i * N:(i + 1) * N] for t in act)
                        col, stride, lo = (W_QKV, 3 * D, 2 * D) if s == SELF else (W_KV, 2 * D, D)
                        mm = product(dst[:, 0:D], act, w(col, c, stride, lo, D), c == 0, c == CT - 1)
                        continue
                    col, stride, lo = {("q", SELF): (W_QKV, 3 * D, 0), ("k", SELF): (W_QKV, 3 * D, D),
                                       ("q", CROSS): (W_Q, D, 0), ("k", CROSS): (W_KV, 2 * D, 0),
                                       ("f", None): (W_F1, DF, 0)}[kind, s]
                    mm = product(dst[:], w(col, c, stride, lo + i * P, P), act, c == 0, c == CT - 1)
                mm.then_inc(tile_full, 1)

            def scores(it, layer, s, g):
                b, q = divmod(g, QUADS)
                if g == 0:
                    if layer == 0:
                        for kind in "kq":
                            for t in range(CT):
                                moved_by(pe, it, tile_of(s, kind, t))
                    else:
                        pe.wait_ge(keys_made, (it - NG) * 4 + 2 * s + 2)
                        pe.wait_ge(queries_made, (it - NG) * 4 + 2 * s + 2)
                        
                if g < 2:
                    moved_by(pe, it, 8 * s + RING + g)
                else:
                    pe.wait_ge(exps_made, it * 32 + s * STEPS + g - 1)
                dst = ring[g % 2]
                r = slice(32 * q, 32 * q + 32)
                masked = layer == 0 and s == CROSS
                if masked:
                    if g == 0:
                        pe.wait_ge(mask_made, it + 1)
                    row = mask_row[32 * q:32 * q + 1, b * N:(b + 1) * N].unsqueeze(1).broadcast_to([1, 4, N])
                    pe.matmul(dst[:].rearrange("p (h n) -> p h n", h=4), ones_row[32 * q:32 * q + 1, :], row,
                              start=True, stop=False, skip_group_check=True)
                for t in range(CT):
                    mm = pe.matmul(dst[:, t * 2 * N:(t + 1) * 2 * N].rearrange("p (e n) -> p e n", e=2),
                                   q_t[r, t, b * N:(b + 1) * N], k_t[r, t, :, b * N:(b + 1) * N],
                                   start=not masked, stop=True, skip_group_check=masked)
                mm.then_inc(scored, 1)

            def turn_probs(it, s, g):
                pe.wait_ge(exps_made, it * 32 + s * STEPS + g + 1)
                if g < 2:
                    moved_by(pe, it, 8 * s + RING + 2 + g)
                else:
                    pe.wait_ge(probs_moved, it * 32 + s * STEPS + g - 1)
                for h in range(4):
                    mm = pe.transpose(ring[2 + g % 2][:, h * N:(h + 1) * N], probs[:, g % 3, h, :], ident[:])
                mm.then_inc(probs_turned, 1)

            def mix_values(it, s, b):
                pe.wait_ge(probs_moved, it * 32 + s * STEPS + QUADS * b + QUADS)
                moved_by(pe, it, tile_of(s, "v", b))
                if b >= 2:
                    pe.wait_ge(heads_scaled, it * 8 + 4 * s + b - 1)
                dst = mix[b % 2]
                for t in range(CT):
                    for e in range(2):
                        for q in range(QUADS):
                            mm = pe.matmul(dst[32 * q:32 * q + 32, t * N:(t + 1) * N],
                                           v_pad[:, b, 8 * t + 2 * q + e, :],
                                           probs_t[:, b % 2, q, 2 * t + e, :],
                                           start=(e == 0), stop=(e == 1), tile_position=(0, 32 * q))
                mm.then_inc(mixed, 1)

            def turn_rden(it, s, b):
                pe.wait_ge(rden_spread, it * 8 + 4 * s + b + 1)
                for t in range(CT):
                    mm = pe.transpose(mix[b % 2][:, D + t * P:D + (t + 1) * P], rden_wide[:, t * P:(t + 1) * P], ident[:])
                mm.then_inc(rden_turned, 1)

            def project(it, s, b):
                j = 4 * s + b
                pe.wait_ge(heads_hi_made, it * 8 + j + 1)
                pe.wait_ge(heads_lo_made, it * 8 + j + 1)
                if j:
                    pe.wait_ge(y_moved, it * 12 + j)
                for t in range(CT):
                    mm = product(p_proj[:, 0:D], (heads_hi[:, b % 2, t, :], heads_lo[:, b % 2, t, :]),
                                 w(W_SA if s == SELF else W_CA, t, D, 0, D), t == 0, t == CT - 1)
                mm.then_inc(projected, 1)

            def fc2(it, f):
                pe.wait_ge(hid_hi_made, it * 8 + f + 1)
                pe.wait_ge(hid_lo_made, it * 8 + f + 1)
                slot = f % HID_SLOTS
                for b in range(GB):
                    cols = slice(b * N, (b + 1) * N)
                    mm = product(y_mlp[b][:, 0:D], (hid_hi[:, slot, cols], hid_lo[:, slot, cols]),
                                 w(W_F2, f, D, 0, D), f == 0, f == FT - 1)
                    if f == FT - 1:
                        mm.then_inc(fc2_full, 1)
                if f < FT - HID_SLOTS:
                    mm.then_inc(hid_used, 1)

            def attention(it, layer, s, between):
                for step in range(LAST_STEP + 1):
                    if step < STEPS:
                        scores(it, layer, s, step)
                    if 0 <= step - AT_TURN < STEPS:
                        turn_probs(it, s, step - AT_TURN)
                    if (b := batch_at(step, AT_MIX)) is not None:
                        mix_values(it, s, b)
                        turn_rden(it, s, b)
                    if (b := batch_at(step, AT_PROJ)) is not None:
                        project(it, s, b)
                    if (b := batch_at(step, AT_LNT)) is not None:
                        turn_z(it, s + 1, b)
                    for n in between.get(step, ()):
                        big_tile(it, n)

            pe.wait_ge(c_loaded, 16 * (CONST_LOADS - 1))
            pe.wait_ge(silu_step, 4)
            ada = stage[:, 0:CT * 6 * D].rearrange("p (t n) -> p t n", t=CT)
            lnw = [k_t[:].rearrange("p t e n -> p (t e n)").rearrange("p (m t n) -> p m t n", m=2, t=CT)[:, m]
                   for m in range(2)] + [q_t[:]]
            n = 0
            for chunk in (1, 0, 4, 3):
                for o in range(CT):
                    for c in range(CT):
                        mm = pe.matmul(mix[0][:, n * B:(n + 1) * B],
                                       ada[:, c, chunk * D + o * P:chunk * D + (o + 1) * P], silu[:, c, :],
                                       start=(c == 0), stop=(c == CT - 1))
                    n += 1
            for g, chunk in enumerate((2, 5)):
                for c in range(CT):
                    mm = pe.matmul(p_proj[0:B, g * D:(g + 1) * D], silu[:, c, :],
                                   ada[:, c, chunk * D:(chunk + 1) * D], start=(c == 0), stop=(c == CT - 1))
            mm.then_inc(mod_full, 1)
            n = 0
            for k in range(3):
                for half in range(2):
                    for o in range(CT):
                        for c in range(CT):
                            mm = pe.matmul(mix[1][:, n * B:(n + 1) * B],
                                           lnw[k][:, c, half * D + o * P:half * D + (o + 1) * P], cond[:, c, :],
                                           start=(c == 0), stop=(c == CT - 1))
                        n += 1
            mm.then_inc(mod_full, 1)

            for layer in range(LAYERS):
                pe.wait_ge(w_hi_made, 4 * layer + 4)
                pe.wait_ge(w_lo_made, 4 * layer + 4)
                with pe.Fori(0, NG) as i:
                    it = i + layer * NG
                    for b in range(GB):
                        turn_z(it, 0, b)
                    for n in range(8):
                        big_tile(it, n)
                    attention(it, layer, SELF, {18: (8, 9), 20: (10, 11, 12, 13), LAST_STEP: (14, 15)})
                    attention(it, layer, CROSS, {})
                    for f in range(HID_SLOTS):
                        big_tile(it, 16 + f)
                    for f in range(FT):
                        fc2(it, f)
                        if f + HID_SLOTS < FT:
                            big_tile(it, 16 + f + HID_SLOTS)

        @block.scalar
        def _(act):
            def modulate(it, k, b):
                act.wait_ge(z_turned, it * 12 + 4 * k + b + 1)
                if 4 * k + b >= 2:
                    act.wait_ge(xt_lo_made, it * 12 + 4 * k + b - 1)
                for c in range(CT):
                    m = (k * CT + c) * 2
                    op = act.activation(xt[:, b % 2, c, :], p_ln[:, c * P:(c + 1) * P], ACT.Identity,
                                        scale=mod_now[:, m, b:b + 1], bias=mod_now[:, m + 1, b:b + 1])
                op.then_inc(ln_moved, 1)
                act.wait_ge(ln_moved, it * 12 + 4 * k + b + 1)
                act.copy(xt_hi[:, :, b * N:(b + 1) * N], xt[:, b % 2, :, :]).then_inc(xt_hi_made, 1)

            def move_tile(it, layer, n):
                s, kind, i = TILES[n]
                j = {SELF: 0, CROSS: 4, None: 0}[s] + {"k": 0, "q": 2}.get(kind, 0) + i
                if kind == "f":
                    act.wait_ge(tile_full, it * len(TILES) + n + 1)
                    if i >= 2:
                        act.wait_ge(hid_lo_made, it * 8 + i - 1)
                    act.activation(hid[:, i % 2, :], ring[n % RING][:], ACT.Gelu,
                                   bias=bias_cols[:, 8 + FT * layer + i:9 + FT * layer + i]).then_inc(moved[n % RING], 1)
                elif layer == 0 and kind == "q":
                    act.wait_ge(tile_full, it * len(TILES) + n + 1)
                    m = 4 + 2 * s + i
                    act.activation(q_t[:, i, :], ring[n % RING][:], ACT.Identity, scale=SCALE,
                                   bias=bias_cols[:, m:m + 1]).then_inc(moved[n % RING], 1)
                elif layer == 1 and kind in "kq":
                    act.wait_ge(tile_full, it * len(TILES) + n + 1)
                    if j >= 2:
                        act.wait_ge(shuffled, (it - NG) * 8 + j - 1)
                        act.wait_ge(cos_made, (it - NG) * 8 + j - 1)
                    act.activation(raw[:, j % 2, :], ring[n % RING][:], ACT.Copy,
                                   scale=SCALE if kind == "q" else 1.0).then_inc(moved[n % RING], 1)

            def exps(it, s, g):
                b, q = divmod(g, QUADS)
                act.wait_ge(max_made, it * 32 + s * STEPS + g + 1)
                if g >= 3:
                    act.wait_ge(probs_turned, it * 32 + s * STEPS + g - 2)
                for h in range(4):
                    head = 8 * (h // 2) + 2 * q + h % 2
                    op = act.activation(probs[:, g % 3, h, :], ring[g % 2][:, h * N:(h + 1) * N], ACT.Exp,
                                        bias=neg_max[:, g % 2, h:h + 1], accum_out=row_sum[:, b % 2, head:head + 1])
                op.then_inc(exps_made, 1)

            def move_rden(it, s, b):
                act.wait_ge(rden_turned, it * 8 + 4 * s + b + 1)
                act.copy(rden_t[:], mix[b % 2][:, D:2 * D]).then_inc(rden_moved, 1)

            def split_heads(it, s, b):
                act.wait_ge(heads_scaled, it * 8 + 4 * s + b + 1)
                act.copy(heads_hi[:, b % 2], heads[:, b % 2]).then_inc(heads_hi_made, 1)

            def attention(it, layer, s, between):
                for step in range(LAST_STEP + 1):
                    if step < STEPS:
                        exps(it, s, step)
                    if (b := batch_at(step, AT_MIX)) is not None:
                        move_rden(it, s, b)
                    if (b := batch_at(step, AT_SCALE)) is not None:
                        split_heads(it, s, b)
                    if (b := batch_at(step, AT_LNT)) is not None:
                        modulate(it, s + 1, b)
                    for n in between.get(step, ()):
                        move_tile(it, layer, n)

            act.wait_ge(c_loaded, 16 * (CONST_LOADS - 1))
            act.activation(silu_tmp[:], cond[:], ACT.Exp, scale=-1.0).then_inc(silu_step, 1)
            for layer in range(LAYERS):
                for c in range(4):
                    n = 4 * layer + c
                    act.wait_ge(w_loaded[c % 2], 16 * W_LOADS[n])
                    act.copy(w_hi[:, c * CHUNK:(c + 1) * CHUNK], stage[:, (c % 2) * CHUNK:(c % 2 + 1) * CHUNK])\
                       .then_inc(w_hi_made, 1)
                with act.Fori(0, NG) as i:
                    it = i + layer * NG
                    act.wait_ge(ctx_loaded, (it + 1) * 16)
                    act.copy(ctx_hi[:], ctxt[:]).then_inc(ctx_hi_made, 1)
                    act.wait_ge(mod_copied, it + 1)
                    for b in range(GB):
                        modulate(it, 0, b)
                    for n in range(8):
                        move_tile(it, layer, n)
                    attention(it, layer, SELF, {18: (8, 9), 20: (10, 11, 12, 13), LAST_STEP: (14, 15)})
                    attention(it, layer, CROSS, {})
                    for n in range(16, 24):
                        move_tile(it, layer, n)

        @block.vector
        def _(dve):
            def moments(it, layer, k, b):
                j = 4 * k + b
                if k == 0:
                    dve.wait_ge(x_loaded, (it + 1) * 16)
                else:
                    x_ready(dve, layer, it - layer * NG, j - 4)
                src = x_new if k == 0 else x
                dve.bn_stats(stats[:, b, :], src[:, b, :]).then_inc(stats_made, 1)
                dve.wait_ge(stats_made, it * 12 + j + 1)
                dve.sem_inc(dve_held, 1)
                dve.bn_aggr(mean_var[:, b, :], stats[:, b, :]).then_inc(moments_made, 1)

            def normalise(it, k, b):
                dve.wait_ge(rstd_made, it * 12 + 4 * k + b + 1)
                src = x_new if k == 0 else x
                dve.tensor_scalar(z[:, b, :], src[:, b, :], mean_var[:, b, 0:1], rstd[:, b:b + 1],
                                  ALU.subtract, ALU.mult).then_inc(z_made, 1)

            def move_tile(it, layer, n):
                s, kind, i = TILES[n]
                src = ring[n % RING]
                if kind == "v":
                    dve.wait_ge(tile_full, it * len(TILES) + n + 1)
                    flat = v_pad[:, i].rearrange("p h w -> p (h w)").rearrange("p (a e w) -> p a e w", a=H // 2, e=2)
                    for e in range(2):
                        dst = flat[:, :, e, e * HD:(e + 1) * HD]
                        heads_of = src[:, 0:D].rearrange("p (a e d) -> p a e d", a=H // 2, e=2)[:, :, e, :]
                        if layer == 0:
                            bias = bias_rows[:, s, :].rearrange("p (a e d) -> p a e d", a=H // 2, e=2)[:, :, e, :]
                            op = dve.tensor_tensor(dst, heads_of, bias, ALU.add)
                        else:
                            op = dve.tensor_copy(dst, heads_of)
                    op.then_inc(moved[n % RING], 1)
                elif layer == 0 and kind == "k":
                    dve.wait_ge(tile_full, it * len(TILES) + n + 1)
                    m = 2 * s + i
                    for e in range(2):
                        op = dve.tensor_scalar(k_t[:, i, e, :], src[:], bias_cols[:, m:m + 1], head_mask[:, e:e + 1],
                                               ALU.add, ALU.mult)
                    op.then_inc(moved[n % RING], 1)
                elif layer == 1 and kind in "kq":
                    g = it - NG
                    j = 4 * s + (2 if kind == "q" else 0) + i
                    r0 = 6 * s + (i * 2 if kind == "k" else 4 + i)
                    moved_by(dve, it, n)
                    if j >= 1:
                        if kind == "q" and i == 1:
                            dve.wait_ge(queries_made, g * 4 + 2 * s + 1)
                        elif kind == "k" and s == 1 and i == 0:
                            dve.wait_ge(queries_made, g * 4 + 2)
                        else:
                            dve.wait_ge(keys_made, g * 4 + 2 * s + (i if kind == "k" else 2))
                    dve.sem_inc(dve_held, 1)
                    dve.stream_shuffle(rot[:], raw[:, j % 2, :], SWAP).then_inc(shuffled, 1)
                    dve.wait_ge(shuffled, g * 8 + j + 1)
                    table = sin_t[:].unsqueeze(1).broadcast_to([P, GB, N])
                    rot3 = rot[:].rearrange("p (b n) -> p b n", b=GB)
                    dve.tensor_tensor(rot3, rot3, table, ALU.mult).then_inc(rot_step, 1)
                    if kind == "k":
                        dve.wait_ge(rot_step, g * 12 + r0 + 1)
                        dve.wait_ge(cos_made, g * 8 + j + 1)
                        dve.tensor_tensor(rot[:], straight[:, j % 2, :], rot[:], ALU.add).then_inc(rot_step, 1)
                        dve.wait_ge(rot_step, g * 12 + r0 + 2)
                        for e in range(2):
                            op = dve.tensor_scalar(k_t[:, i, e, :], rot[:], head_mask[:, e:e + 1], None, ALU.mult)
                        op.then_inc(keys_made, 1)

            def row_max(it, s, g):
                dve.wait_ge(scored, it * 32 + s * STEPS + g + 1)
                dve.tensor_reduce(neg_max[:, g % 2, :], ring[g % 2][:].rearrange("p (h n) -> p h n", h=4),
                                  AX.X, ALU.max, negate=True).then_inc(max_made, 1)

            def move_probs(it, s, g):
                b, q = divmod(g, QUADS)
                dve.wait_ge(probs_turned, it * 32 + s * STEPS + g + 1)
                dve.tensor_copy(probs_t[:, b % 2, q].rearrange("p h n -> p (h n)"), ring[2 + g % 2][:])\
                   .then_inc(probs_moved, 1)

            def make_rden(it, s, b):
                j = 4 * s + b
                dve.wait_ge(exps_made, it * 32 + s * STEPS + QUADS * b + QUADS)
                dve.reciprocal(rden[:, b % 2, :], row_sum[:, b % 2, :]).then_inc(rden_made, 1)
                dve.wait_ge(rden_made, it * 8 + j + 1)
                dve.tensor_copy(rden_wide[:].rearrange("p (h d) -> p h d", h=H),
                                rden[:, b % 2, :].unsqueeze(2).broadcast_to([P, H, HD])).then_inc(rden_spread, 1)

            def scale_heads(it, s, b):
                j = 4 * s + b
                dve.wait_ge(mixed, it * 8 + j + 1)
                dve.wait_ge(rden_moved, it * 8 + j + 1)
                dve.tensor_tensor(heads[:, b % 2].rearrange("p t n -> p (t n)"), mix[b % 2][:, 0:D], rden_t[:],
                                  ALU.mult).then_inc(heads_scaled, 1)

            def take_output(it, layer, j):
                b = j % 4
                if j < 8:
                    dve.wait_ge(projected, it * 8 + j + 1)
                    src = p_proj[:, 0:D]
                else:
                    dve.wait_ge(fc2_full, it * 4 + b + 1)
                    src = y_mlp[b][:, 0:D]
                if layer == 1 and j < 8:
                    if j == 0:
                        dve.wait_ge(stored, it * 16 + 16 * GATE_STORES)
                    dve.tensor_tensor(x[:, b, :], src, x_new[:, b, :] if j < 4 else x[:, b, :], ALU.add)\
                       .then_inc(y_moved, 1)
                else:
                    if j >= 2:
                        if layer == 0:
                            dve.wait_ge(x_updated, it * 12 + j - 1)
                        elif j >= 10:
                            dve.wait_ge(x_updated, (it - NG) * 4 + 12 * NG + j - 9)
                    row = {0: 2, 1: 3, 2: 4}[j // 4] if layer == 0 else 5
                    dve.tensor_tensor(delta[:, j % 2, :], src, bias_rows[:, row, :], ALU.add).then_inc(y_moved, 1)

            def attention(it, layer, s, between):
                for step in range(LAST_STEP + 1):
                    if step < STEPS:
                        row_max(it, s, step)
                    if 0 <= step - AT_TURN < STEPS:
                        move_probs(it, s, step - AT_TURN)
                    if (b := batch_at(step, AT_RDEN)) is not None:
                        make_rden(it, s, b)
                    if (b := batch_at(step, AT_SCALE)) is not None:
                        scale_heads(it, s, b)
                    if (b := batch_at(step, AT_PROJ)) is not None:
                        take_output(it, layer, 4 * s + b)
                    if (b := batch_at(step, AT_STATS)) is not None:
                        moments(it, layer, s + 1, b)
                    if (b := batch_at(step, AT_Z)) is not None:
                        normalise(it, s + 1, b)
                    for n in between.get(step, ()):
                        move_tile(it, layer, n)

            dve.memset(ones_row[:], 1.0).then_inc(ready, 1)
            dve.memset(v_pad[:], 0.0).then_inc(ready, 1)
            dve.memset(mod[:, 0, 1, :, 0, :], 1.0).then_inc(ready, 1)
            dve.memset(mod[:, 0, 1, :, 1, :], 0.0).then_inc(ready, 1)
            dve.wait_ge(silu_step, 1)
            dve.tensor_scalar(silu_tmp[:], silu_tmp[:], 1.0, None, ALU.add).then_inc(silu_step, 1)
            dve.wait_ge(silu_step, 2)
            dve.reciprocal(silu_tmp[:], silu_tmp[:]).then_inc(silu_step, 1)
            dve.wait_ge(silu_step, 3)
            dve.tensor_tensor(silu[:], cond[:], silu_tmp[:], ALU.mult).then_inc(silu_step, 1)
            dve.tensor_scalar(bias_cols[:, 4:8], bias_cols[:, 4:8], SCALE, None, ALU.mult).then_inc(ready, 1)
            dve.wait_ge(mod_full, 1)
            for m, k in enumerate((0, 2)):
                dve.tensor_tensor(mod[:, 0, k].rearrange("p c s b -> p s c b"),
                                  mix[0][:, m * 4 * B:(m + 1) * 4 * B].rearrange("p (s c b) -> p s c b", s=2, c=CT),
                                  bias_mod[:, 4 * m:4 * m + 4].rearrange("p (s c) -> p s c", s=2).unsqueeze(3)
                                  .broadcast_to([P, 2, CT, B]), ALU.add).then_inc(mod_step, 1)
            dve.tensor_tensor(gate_rows[:].rearrange("b g c -> b (g c)"), p_proj[0:B, :],
                              gate_bias[:].rearrange("b g c -> b (g c)"), ALU.add).then_inc(gates_made, 1)
            dve.wait_ge(mod_full, 2)
            for k in range(3):
                dve.tensor_tensor(mod[:, 1, k].rearrange("p c s b -> p s c b"),
                                  mix[1][:, k * 4 * B:(k + 1) * 4 * B].rearrange("p (s c b) -> p s c b", s=2, c=CT),
                                  bias_mod[:, 8 + 4 * k:12 + 4 * k].rearrange("p (s c) -> p s c", s=2).unsqueeze(3)
                                  .broadcast_to([P, 2, CT, B]), ALU.add).then_inc(mod_step, 1)
            dve.wait_ge(mod_step, 5)
            for m, (layer, k) in enumerate(((0, 0), (0, 2), (1, 0), (1, 1), (1, 2))):
                dve.tensor_scalar(mod[:, layer, k, :, 0, :], mod[:, layer, k, :, 0, :], 1.0, None, ALU.add)\
                   .then_inc(mod_step, 1)
            dve.wait_ge(mod_step, 10)
            dve.wait_ge(ready, 5)

            for layer in range(LAYERS):
                for c in range(4):
                    n = 4 * layer + c
                    dve.wait_ge(w_hi_made, n + 1)
                    dve.tensor_tensor(w_lo[:, c * CHUNK:(c + 1) * CHUNK], stage[:, (c % 2) * CHUNK:(c % 2 + 1) * CHUNK],
                                      w_hi[:, c * CHUNK:(c + 1) * CHUNK].bitcast(F32), ALU.subtract).then_inc(w_lo_made, 1)
                with dve.Fori(0, NG) as i:
                    it = i + layer * NG
                    dve.tensor_copy(mod_now[:], mod[:, layer].rearrange("p k c s b -> p (k c s) b")[:, :, bass.ds(i * GB, GB)])\
                       .then_inc(mod_copied, 1)
                    for b in range(GB):
                        moments(it, layer, 0, b)
                        if b:
                            normalise(it, 0, b - 1)
                    normalise(it, 0, GB - 1)
                    if layer == 0:
                        dve.wait_ge(side_loaded, (i + 1) * 32)
                        dve.tensor_scalar(mask_row[:], mask_u8[:], MASKED, None, ALU.mult).then_inc(mask_made, 1)
                    for n in range(8):
                        move_tile(it, layer, n)
                    attention(it, layer, SELF, {18: (8, 9), 20: (10, 11, 12, 13), LAST_STEP: (14, 15)})
                    attention(it, layer, CROSS, {})
                    for f in range(FT):
                        moved_by(dve, it, 16 + f)
                        if f >= HID_SLOTS:
                            dve.wait_ge(hid_used, it * 4 + f - HID_SLOTS + 1)
                        dve.tensor_copy(hid_hi[:, f % HID_SLOTS, :], hid[:, f % 2, :]).then_inc(hid_hi_made, 1)
                    for b in range(GB):
                        take_output(it, layer, 8 + b)

        @block.gpsimd
        def _(pool):
            def make_rstd(it, layer, k, b):
                j = 4 * k + b
                pool.wait_ge(moments_made, it * 12 + j + 1)
                pool.sem_inc(pool_held, 1)
                pool.tensor_scalar(var_eps[:, b:b + 1], mean_var[:, b, 1:2], EPS[layer], None, ALU.add).then_inc(eps_added, 1)
                pool.wait_ge(eps_added, it * 12 + j + 1)
                pool.tensor_tensor(rstd[:, b:b + 1], var_eps[:, b:b + 1], minus_half[:], ALU.pow).then_inc(rstd_made, 1)

            def split_xt(it, k, b):
                pool.wait_ge(xt_hi_made, it * 12 + 4 * k + b + 1)
                cols = slice(b * N, (b + 1) * N)
                pool.tensor_tensor(xt_lo[:, :, cols], xt[:, b % 2], xt_hi[:, :, cols].bitcast(F32), ALU.subtract)\
                    .then_inc(xt_lo_made, 1)

            def split_heads(it, s, b):
                pool.wait_ge(heads_hi_made, it * 8 + 4 * s + b + 1)
                pool.tensor_tensor(heads_lo[:, b % 2], heads[:, b % 2], heads_hi[:, b % 2].bitcast(F32), ALU.subtract)\
                    .then_inc(heads_lo_made, 1)

            def add_output(it, layer, j):
                b = j % 4
                if layer == 1 and j < 8:
                    return
                pool.wait_ge(y_moved, it * 12 + j + 1)
                if layer == 0 and not 4 <= j < 8:
                    g = j // 8
                    if j == 0:
                        pool.wait_ge(side_loaded, (it + 1) * 32)
                    pool.tensor_tensor(delta[:, j % 2, :], delta[:, j % 2, :], gate_now[:, b, g, :], ALU.mult)\
                        .then_inc(gated, 1)
                    pool.wait_ge(gated, it * 8 + (j if j < 4 else j - 4) + 1)
                if j == 0:
                    pool.wait_ge(stored, it * 16 + 16 * GATE_STORES)
                pool.tensor_tensor(x[:, b, :], x_new[:, b, :] if j < 4 else x[:, b, :], delta[:, j % 2, :], ALU.add)\
                    .then_inc(x_updated, 1)

            def rope_tile(it, n):
                s, kind, i = TILES[n]
                if kind not in "kq":
                    return
                g = it - NG
                j = 4 * s + (2 if kind == "q" else 0) + i
                moved_by(pool, it, n)
                if kind == "q":
                    pool.wait_ge(keys_made, g * 4 + 2 * s + i + 1)
                table = cos_t[:].unsqueeze(1).broadcast_to([P, GB, N])
                pool.tensor_tensor(straight[:, j % 2, :].rearrange("p (b n) -> p b n", b=GB),
                                   raw[:, j % 2, :].rearrange("p (b n) -> p b n", b=GB), table, ALU.mult)\
                    .then_inc(cos_made, 1)
                if kind == "q":
                    pool.wait_ge(cos_made, g * 8 + j + 1)
                    pool.wait_ge(rot_step, g * 12 + 6 * s + 4 + i + 1)
                    pool.tensor_tensor(q_t[:, i, :], straight[:, j % 2, :], rot[:], ALU.add).then_inc(queries_made, 1)

            def attention(it, layer, s, between):
                for step in range(LAST_STEP + 1):
                    if (b := batch_at(step, AT_SCALE)) is not None:
                        split_heads(it, s, b)
                    if (b := batch_at(step, AT_PROJ)) is not None:
                        add_output(it, layer, 4 * s + b)
                    if (b := batch_at(step, AT_STATS)) is not None:
                        make_rstd(it, layer, s + 1, b)
                    if (b := batch_at(step, AT_LNT)) is not None:
                        split_xt(it, s + 1, b)
                    if layer == 1:
                        for n in between.get(step, ()):
                            rope_tile(it, n)

            pool.memset(minus_half[:], -0.5).then_inc(half_made, 1)
            for layer in range(LAYERS):
                with pool.Fori(0, NG) as i:
                    it = i + layer * NG
                    for b in range(GB):
                        make_rstd(it, layer, 0, b)
                    for b in range(GB):
                        split_xt(it, 0, b)
                    pool.wait_ge(ctx_hi_made, it + 1)
                    pool.tensor_tensor(ctx_lo[:], ctxt[:], ctx_hi[:].bitcast(F32), ALU.subtract).then_inc(ctx_lo_made, 1)
                    if layer == 1:
                        for n in range(8):
                            rope_tile(it, n)
                    attention(it, layer, SELF, {18: (8, 9), 20: (10, 11, 12, 13), LAST_STEP: (14, 15)})
                    attention(it, layer, CROSS, {})
                    for f in range(FT):
                        pool.wait_ge(hid_hi_made, it * 8 + f + 1)
                        pool.tensor_tensor(hid_lo[:, f % HID_SLOTS, :], hid[:, f % 2, :],
                                           hid_hi[:, f % HID_SLOTS, :].bitcast(F32), ALU.subtract)\
                            .then_inc(hid_lo_made, 1)
                    for b in range(GB):
                        add_output(it, layer, 8 + b)


SWAP = [16 * (p // 16) + (p % 16 + HD // 2) % HD for p in range(32)]

WEIGHTS = [
    [[("L0_xcond_qkv_w", W_QKV, CT, 3 * D), ("L0_xcond_sa_proj_w", W_SA, CT, D)],
     [("L0_xcond_q_w", W_Q, CT, D), ("L0_xcond_kv_w", W_KV, CT, 2 * D), ("L0_xcond_ca_proj_w", W_CA, CT, D)],
     [("L0_xcond_fc1_w", W_F1, CT, DF)],
     [("L0_xcond_fc2_w", W_F2, FT, D)]],
    [[("L1_qkv_wT", W_QKV, CT, 3 * D), ("L1_sa_wT", W_SA, CT, D)],
     [("L1_q_wT", W_Q, CT, D), ("L1_kv_wT", W_KV, CT, 2 * D), ("L1_ca_wT", W_CA, CT, D)],
     [("L1_f1_wT", W_F1, CT, DF)],
     [("L1_f2_wT", W_F2, FT, D)]],
]
_PARTS = [len(c) for layer in WEIGHTS for c in layer]
W_LOADS = [sum(_PARTS[n % 2:n + 1:2]) for n in range(len(_PARTS))]


def rope_tables():
    half = HD // 2
    inv = (1.0 / np.float32(10000.0) ** (np.arange(half, dtype=np.float32) / np.float32(half))).astype(np.float32)
    ang = np.arange(N, dtype=np.float32)[None, :] * inv[:, None]
    cos, sin = np.cos(ang), np.sin(ang)
    return np.tile(cos, (P // half, 1)), np.tile(np.concatenate([-sin, sin]), (P // HD, 1))


def kernel(**inputs):
    import concourse.bacc as bacc
    from concourse.bass_utils import run_bass_kernel_spmd as run

    get = {k: np.asarray(v) for k, v in inputs.items()}
    cols = lambda v: v.reshape(-1, P).T
    zeros = np.zeros
    ada_b = get["L0_xcond_ada_b"].reshape(6, D)
    qkv_b = get["L0_xcond_qkv_b"].reshape(3, D)
    kv_b = get["L0_xcond_kv_b"].reshape(2, D)
    cos, sin = rope_tables()
    arrays = {
        "x": get["x"].reshape(B * N, D),
        "condT": get["cond_1024"].T,
        "ctxT": get["ctx_1024"].reshape(B * N, D).T,
        "mask": get["mask_BxS2_bf0"].reshape(B * N).view(np.uint32),
        "L0_xcond_ada_w": get["L0_xcond_ada_w"],
        "ln_wT": np.stack([get[f"L1_xcond_ln{k}_w"].T for k in (1, 2, 3)]),
        "bias_mod": np.concatenate([cols(ada_b[c]) for c in (1, 0, 4, 3)]
                                   + [cols(get[f"L1_xcond_ln{k}_b"]) for k in (1, 2, 3)], axis=1),
        "gate_bias": np.stack([ada_b[2], ada_b[5]]),
        "ident": np.eye(P, dtype=np.float32),
        "head_mask": np.stack([np.arange(P) % 32 < HD, np.arange(P) % 32 >= HD], axis=1).astype(np.float32),
        "cos_t": cos,
        "sin_t": sin,
        "bias_rows": np.stack([qkv_b[2], kv_b[1], get["L0_xcond_sa_proj_b"], get["L0_xcond_ca_proj_b"],
                               get["L0_xcond_fc2_b"], get["L1_xcond_ffn_b2"]]),
        "bias_cols": np.concatenate([cols(qkv_b[1]), cols(kv_b[0]), cols(qkv_b[0]), cols(get["L0_xcond_q_b"]),
                                     cols(get["L0_xcond_fc1_b"]), cols(get["L1_xcond_ffn_b1"])], axis=1),
        "L1_qkv_wT": get["L1_xcond_qkv_w"].T,
        "L1_sa_wT": get["L1_xcond_sa_out_w"].T,
        "L1_q_wT": get["L1_xcond_q_w"].T,
        "L1_kv_wT": np.concatenate([get["L1_xcond_k_w"].T, get["L1_xcond_v_w"].T], axis=1),
        "L1_ca_wT": get["L1_xcond_ca_out_w"].T,
        "L1_f1_wT": get["L1_xcond_ffn_w1"].T,
        "L1_f2_wT": get["L1_xcond_ffn_w2"].T,
    }
    for name in ("qkv", "sa_proj", "q", "kv", "ca_proj", "fc1", "fc2"):
        arrays[f"L0_xcond_{name}_w"] = get[f"L0_xcond_{name}_w"]
    arrays = {k: np.ascontiguousarray(v) for k, v in arrays.items()}

    nc = bacc.Bacc("TRN2", target_bir_lowering=False, num_devices=1)
    a = {k: nc.dram_tensor(f"in_{k}", v.shape, mybir.dt.from_np(v.dtype), kind="ExternalInput").ap()
         for k, v in arrays.items()}
    x_mid = nc.dram_tensor("x_mid", (B * N, D), F32, kind="Internal").ap()
    gates = nc.dram_tensor("gates", (B, 2, D), F32, kind="Internal").ap()
    out = nc.dram_tensor("out", (B * N, D), F32, kind="ExternalOutput").ap()
    build_blocks(nc, a, x_mid, gates, out)
    r = run(nc, [{f"in_{k}": v for k, v in arrays.items()}], core_ids=[0])
    return r.results[0]["out"].reshape(B, N, D)
```

```python
from contextlib import ExitStack

import numpy as np
import concourse.bass as bass
from concourse import mybir

F32 = mybir.dt.float32
F32R = mybir.dt.float32r
BF16 = mybir.dt.bfloat16
U8 = mybir.dt.uint8
U32 = mybir.dt.uint32
ALU = mybir.AluOpType
ACT = mybir.ActivationFunctionType
AX = mybir.AxisListType

P = 128
B, N, D, H = 32, 128, 256, 16
HD = D // H
DF = 4 * D
CT = D // P
FT = DF // P
GB = 4
NG = B // GB
GN = GB * N
LAYERS = 2
EPS = (1e-6, 1e-5)
SCALE = HD ** -0.5
MASKED = -1e30
QUADS = 4
STEPS = GB * QUADS
SELF, CROSS = 0, 1

W_QKV = 0
W_SA = W_QKV + CT * 3 * D
W_Q = W_SA + CT * D
W_KV = W_Q + CT * D
W_CA = W_KV + CT * 2 * D
W_F1 = W_CA + CT * D
W_F2 = W_F1 + CT * DF
W_ALL = W_F2 + FT * D
CHUNK = W_ALL // 4

RING = 4
P_PROJ = RING
FIRST = {("q", 0, 0): 2, ("k", 0, 0): 3, ("v", 0, 0): 1}
HALF = GN // 2
HIDDEN = 2 * FT
MLP_RING = 3
HID_SLOTS = 4

AT_TURN = 2
AT_RDEN, AT_MIX, AT_SCALE, AT_PROJ, AT_STATS, AT_Z, AT_LNT = 4, 6, 7, 9, 10, 11, 12
CROSS_FROM = 21
AT_MASK = 10
LAST_STEP = CROSS_FROM + QUADS * (GB - 1) + AT_LNT
SIDE = {-1: (("v", 0, 1), P_PROJ), 1: (("k", 0, 1), P_PROJ), 3: (("q", 0, 1), P_PROJ), 11: (("k", 1, 0), P_PROJ),
        17: (("v", 1, 1), 0), 18: (("q", 1, 0), 1), 19: (("k", 1, 1), 2), 20: (("v", 1, 0), 3),
        26: (("q", 1, 1), P_PROJ)}
ACT_KEYS = ("k", 0, 1)
UNITS = list(FIRST) + [unit for unit, _ in SIDE.values()]
IN_BANK = [[u for u, r in list(FIRST.items()) + list(SIDE.values()) if r == bank] for bank in range(RING + 1)]
MOVED = [len(units) + len(range(r, HIDDEN, MLP_RING)) * (r < MLP_RING)
         for r, units in enumerate(IN_BANK)]
ROPED = [u for u in UNITS if u[0] != "v"]
SWAP_LAG, MASK_LAG = 1, 4
AT_CTX = 6
SIDE_STEPS = sorted(SIDE)


def mlp_order(half):
    u = [("up", f) for f in range(HID_SLOTS)]
    for f in range(FT):
        u.append(("down", f))
        if f + HID_SLOTS < FT:
            u.append(("up", f + HID_SLOTS))
    return [(kind, FT * half + f) for kind, f in u]


FIRST_HALF, _rest = {}, mlp_order(0)
for _step, _n in zip(range(CROSS_FROM + 17, LAST_STEP + 1), (2, 2, 2, 1, 2, 2, 2, 3)):
    FIRST_HALF[_step], _rest = _rest[:_n], _rest[_n:]
assert not _rest


def batch_at(step, lag):
    for s, start in ((SELF, 0), (CROSS, CROSS_FROM)):
        b, r = divmod(step - start - lag, QUADS)
        if r == 0 and 0 <= b < GB:
            yield s, b


def roped_at(step, lag):
    return [SIDE[t][0] for t in (step - lag,) if t in SIDE and SIDE[t][0] in ROPED]


def quad_at(step, lag):
    for s, start in ((SELF, 0), (CROSS, CROSS_FROM)):
        if 0 <= step - start - lag < STEPS:
            yield s, step - start - lag


def build_blocks(nc, a, x_mid, gates_dram, out):
    ctx = ExitStack()
    with ctx:
        def sb(name, shape, dt=F32):
            return ctx.enter_context(nc.sbuf_tensor(name, shape, dt))

        def bank(name):
            return ctx.enter_context(nc.psum_tensor(name, [P, 512], F32))

        def sem(name):
            return ctx.enter_context(nc.semaphore(name))

        w_hi = sb("w_hi", [P, W_ALL], F32R)
        w_lo = sb("w_lo", [P, W_ALL], F32R)
        ident = sb("ident", [P, P])
        head_mask = sb("head_mask", [P, 2])
        cos_t = sb("cos_t", [P, N])
        sin_t = sb("sin_t", [P, N])
        ones_row = sb("ones_row", [P, P], BF16)
        minus_half = sb("minus_half", [P, 1])
        bias_rows = sb("bias_rows", [P, 6, D])
        bias_cols = sb("bias_cols", [P, 8 + 2 * FT])
        bias_masked = sb("bias_masked", [P, 2, CT])
        bias_mod = sb("bias_mod", [P, 20])
        mod = sb("mod", [P, 13, LAYERS * B + GB])
        mod_first = sb("mod_first", [P, 5, GB])
        mod_now = sb("mod_now", [P, 8, GB])
        eps_cols = sb("eps_cols", [P, LAYERS])
        cond = sb("cond", [P, CT, B])
        silu = sb("silu", [P, CT, B])
        silu_tmp = sb("silu_tmp", [P, CT, B])
        gate_now = sb("gate_now", [P, GB, 2, D])
        mask_u8 = sb("mask_u8", [P, GN], U8)
        mask_row = sb("mask_row", [P, GN], BF16)
        x_new = sb("x_new", [P, GB, D])
        x = sb("x", [P, GB, D])
        stats = sb("stats", [P, GB, 6])
        mean_var = sb("mean_var", [P, GB, 2])
        var_eps = sb("var_eps", [P, GB])
        rstd = sb("rstd", [P, GB])
        z = sb("z", [P, GB, D])
        xt = sb("xt", [P, 2, CT, N])
        xt_hi = sb("xt_hi", [P, CT, GN], F32R)
        xt_lo = sb("xt_lo", [P, CT, GN], F32R)
        ctxt = sb("ctxt", [P, CT, GN])
        ctx_hi = sb("ctx_hi", [P, CT, GN], F32R)
        ctx_lo = sb("ctx_lo", [P, CT, GN], F32R)
        q_t = sb("q_t", [P, CT, GN])
        k_t = [sb(f"k_t{s}", [P, CT, 2, GN]) for s in range(2)]
        v_pad = [sb(f"v_pad{s}", [P, GB, H, 2 * HD]) for s in range(2)]
        raw = sb("raw", [P, 2, GN])
        rot = sb("rot", [P, 2, GN])
        neg_max = sb("neg_max", [P, 2, 4])
        probs = sb("probs", [P, 3, 4, N])
        row_sum = sb("row_sum", [P, 2, H])
        rden = sb("rden", [P, 2, H])
        rden_wide = sb("rden_wide", [P, D])
        rden_t = sb("rden_t", [P, D])
        probs_t = sb("probs_t", [P, 2, QUADS, 4, N])
        heads = sb("heads", [P, 2, CT, N])
        heads_hi = sb("heads_hi", [P, 2, CT, N], F32R)
        heads_lo = sb("heads_lo", [P, 2, CT, N], F32R)
        delta = sb("delta", [P, 2, D])
        gate_bias = raw[0:B, 0, :].rearrange("b (g c) -> b g c", g=2)
        gate_rows = raw[0:B, 1, :].rearrange("b (g c) -> b g c", g=2)
        hid = raw[:, :, 0:HALF]
        hid_hi = sb("hid_hi", [P, HID_SLOTS, HALF], F32R)
        hid_lo = sb("hid_lo", [P, HID_SLOTS, HALF], F32R)
        stage = probs_t[:, :, :, :, :].rearrange("p a q s n -> p (a q s n)")

        ring = [bank(f"ring{r}") for r in range(RING)]
        mix = [bank(f"mix{r}") for r in range(2)]
        p_proj = bank("p_proj")
        p_ln = bank("p_ln")
        y_mlp = [mix[0], ring[3], mix[1], p_proj]

        c_loaded = sem("c_loaded")
        ready = sem("ready")
        dve_held = sem("dve_held")
        half_made = sem("half_made")
        silu_step = sem("silu_step")
        mod_full = sem("mod_full")
        mod_step = sem("mod_step")
        w_loaded = [sem(f"w_loaded{h}") for h in range(2)]
        w_hi_made = sem("w_hi_made")
        w_lo_made = sem("w_lo_made")
        stored = sem("stored")
        x_loaded = sem("x_loaded")
        ctx_loaded = sem("ctx_loaded")
        side_loaded = sem("side_loaded")
        mask_made = sem("mask_made")
        first_copied = sem("first_copied")
        mod_copied = sem("mod_copied")
        ctx_hi_made = sem("ctx_hi_made")
        ctx_lo_made = sem("ctx_lo_made")
        stats_made = sem("stats_made")
        moments_made = sem("moments_made")
        eps_added = sem("eps_added")
        rstd_made = sem("rstd_made")
        z_made = sem("z_made")
        z_turned = sem("z_turned")
        ln_moved = sem("ln_moved")
        xt_hi_made = sem("xt_hi_made")
        xt_lo_made = sem("xt_lo_made")
        first_full = sem("first_full")
        up_full = sem("up_full")
        moved = [sem(f"moved{r}") for r in range(RING)] + [sem("moved_p_proj")]
        side_full = sem("side_full")
        swapped = sem("swapped")
        cos_made = sem("cos_made")
        sin_made = sem("sin_made")
        sin_keys = sem("sin_keys")
        keys_summed = sem("keys_summed")
        keys_made = sem("keys_made")
        queries_made = sem("queries_made")
        scored = sem("scored")
        max_made = sem("max_made")
        exps_made = sem("exps_made")
        probs_turned = sem("probs_turned")
        probs_moved = sem("probs_moved")
        rden_made = sem("rden_made")
        rden_spread = sem("rden_spread")
        mixed = sem("mixed")
        rden_turned = sem("rden_turned")
        rden_moved = sem("rden_moved")
        heads_scaled = sem("heads_scaled")
        heads_hi_made = sem("heads_hi_made")
        heads_lo_made = sem("heads_lo_made")
        projected = sem("projected")
        hid_used = sem("hid_used")
        fc2_full = sem("fc2_full")
        y_moved = sem("y_moved")
        gated = sem("gated")
        x_updated = sem("x_updated")
        hid_hi_made = sem("hid_hi_made")
        hid_lo_made = sem("hid_lo_made")

        GATE_STORES = 1
        CONST_LOADS = 13

        def moved_by(eng, it, unit):
            bank, = (r for r, units in enumerate(IN_BANK) if unit in units)
            eng.wait_ge(moved[bank], it * MOVED[bank] + IN_BANK[bank].index(unit) + 1)

        def up_moved(eng, it, u):
            r = u % MLP_RING
            eng.wait_ge(moved[r], it * MOVED[r] + len(IN_BANK[r]) + u // MLP_RING + 1)

        def y_out(eng, it, j):
            eng.wait_ge(y_moved, it * 12 + 1 + j + 1)

        def x_ready(eng, layer, g, j):
            if layer == 0:
                eng.wait_ge(x_updated, g * 12 + j + 1)
            elif j < 8:
                y_out(eng, g + NG, j)
            else:
                eng.wait_ge(x_updated, g * 4 + 12 * NG + j - 8 + 1)

        block = ctx.enter_context(nc.Block())

        @block.sync
        def _(sp):
            for dst, src in (
                (cond[:], a["condT"].rearrange("(t p) b -> p t b", p=P)),
                (stage[:, 0:CT * 6 * D].rearrange("p (t n) -> p t n", t=CT),
                 a["L0_xcond_ada_w"].rearrange("(t p) n -> p t n", p=P)),
                (k_t[0][:].rearrange("p t e n -> p (t e n)").rearrange("p (m t n) -> p m t n", m=2, t=CT),
                 a["ln_wT"][0:2].rearrange("m (t p) n -> p m t n", p=P)),
                (q_t[:], a["ln_wT"][2].rearrange("(t p) n -> p t n", p=P)),
                (bias_mod[:], a["bias_mod"]),
                (gate_bias, a["gate_bias"].partition_broadcast(B)),
                (ident[:], a["ident"]),
                (head_mask[:], a["head_mask"]),
                (cos_t[:], a["cos_t"]),
                (sin_t[:], a["sin_t"]),
                (bias_rows[:], a["bias_rows"].partition_broadcast(P)),
                (bias_cols[:], a["bias_cols"]),
            ):
                sp.dma_start(dst, src).then_inc(c_loaded, 16)
            sp.dma_start(ctxt[:], a["ctxT"][:, 0:GN].rearrange("(t p) n -> p t n", p=P)).then_inc(ctx_loaded, 16)
            sp.dma_start(x_new[:], a["x"][0:GN, :].rearrange("(b p) c -> p b c", p=P)).then_inc(x_loaded, 16)

            def load_weights(layer):
                for c, parts in enumerate(WEIGHTS[layer]):
                    n = 4 * layer + c
                    if n >= 2 and c >= 2:
                        sp.wait_ge(w_hi_made, n - 1)
                        sp.wait_ge(w_lo_made, n - 1)
                    for name, col, kt, width in parts:
                        at = col - c * CHUNK + (c % 2) * CHUNK
                        dst = stage[:, at:at + kt * width].rearrange("p (t n) -> p t n", t=kt)
                        sp.dma_start(dst, a[name].rearrange("(t p) n -> p t n", p=P)).then_inc(w_loaded[c % 2], 16)

            sp.wait_ge(mod_full, 2)
            load_weights(0)
            sp.wait_ge(y_moved, 1)
            sp.dma_start(gates_dram, gate_rows).then_inc(stored, 16)
            sp.wait_ge(stored, 16)

            def side(i):
                sp.dma_start(gate_now[:].rearrange("p b g c -> p (b g c)"),
                             gates_dram[bass.ds(i * GB, GB)].rearrange("b g c -> (b g c)")
                             .partition_broadcast(P)).then_inc(side_loaded, 16)
                sp.dma_start(mask_u8[:].bitcast(U32), a["mask"][bass.ds(i * (GN // 4), GN // 4)].partition_broadcast(P)).then_inc(side_loaded, 16)

            def load_ctx(i):
                sp.dma_start(ctxt[:], a["ctxT"][:, bass.ds(i * GN, GN)].rearrange("(t p) n -> p t n", p=P))\
                  .then_inc(ctx_loaded, 16)

            def load_x(src, i):
                sp.dma_start(x_new[:], src[bass.ds(i * GN, GN), :].rearrange("(b p) c -> p b c", p=P))\
                  .then_inc(x_loaded, 16)

            def store_x(dst, layer, i):
                x_ready(sp, layer, i, 11)
                sp.dma_start(dst[bass.ds(i * GN, GN), :].rearrange("(b p) c -> p b c", p=P), x[:]).then_inc(stored, 16)

            side(0)
            with sp.Fori(0, NG - 1) as i:
                sp.wait_ge(ctx_lo_made, i + 1)
                load_ctx(i + 1)
                x_ready(sp, 0, i, 3)
                load_x(a["x"], i + 1)
                x_ready(sp, 0, i, 11)
                side(i + 1)
                store_x(x_mid, 0, i)
            sp.wait_ge(ctx_lo_made, NG)
            load_ctx(0)
            x_ready(sp, 0, NG - 1, 3)
            sp.wait_ge(stored, 16 * (GATE_STORES + NG - 1))
            load_x(x_mid, 0)
            sp.wait_ge(mixed, NG * 8)
            load_weights(1)
            x_ready(sp, 0, NG - 1, 11)
            store_x(x_mid, 0, NG - 1)
            sp.wait_ge(stored, 16 * (GATE_STORES + NG))
            with sp.Fori(0, NG - 1) as i:
                sp.wait_ge(ctx_lo_made, i + NG + 1)
                load_ctx(i + 1)
                x_ready(sp, 1, i, 3)
                load_x(x_mid, i + 1)
                store_x(out, 1, i)
            x_ready(sp, 1, NG - 1, 3)
            load_x(x_mid, 0)
            store_x(out, 1, NG - 1)
            sp.wait_ge(stored, 16 * (GATE_STORES + LAYERS * NG))
            sp.wait_ge(x_loaded, 16 * (LAYERS * NG + 1))

        @block.tensor
        def _(pe):
            def product(dst, lhs, rhs, first, last):
                pe.matmul(dst, lhs[1], rhs[0], start=first, stop=False)
                pe.matmul(dst, lhs[0], rhs[1], start=False, stop=False)
                return pe.matmul(dst, lhs[0], rhs[0], start=False, stop=last)

            def w(col, kt, stride, lo, width):
                c = col + kt * stride + lo
                return w_hi[:, c:c + width], w_lo[:, c:c + width]

            def turn_z(it, k, b):
                pe.wait_ge(z_made, it * 12 + 4 * k + b + 1)
                if k > 0:
                    p_ln_free(it, z=True, n=4 * k + b)
                elif not (isinstance(it, int) and b == 0):
                    pe.wait_ge(ln_moved, it * 12 + b)
                for c in range(CT):
                    mm = pe.transpose(p_ln[:, c * P:(c + 1) * P], z[:, b, c * P:(c + 1) * P], ident[:])
                mm.then_inc(z_turned, 1)

            def make_unit(it, unit, dst):
                kind, s, half = unit
                if s == CROSS and kind != "q":
                    pe.wait_ge(ctx_hi_made, it + 1)
                    pe.wait_ge(ctx_lo_made, it + 1)
                    hi, lo = ctx_hi, ctx_lo
                else:
                    pe.wait_ge(xt_hi_made, it * 12 + 4 * s + 2 * half + 2)
                    pe.wait_ge(xt_lo_made, it * 12 + 4 * s + 2 * half + 2)
                    hi, lo = xt_hi, xt_lo
                col, stride, at = {("k", SELF): (W_QKV, 3 * D, D), ("q", SELF): (W_QKV, 3 * D, 0),
                                   ("v", SELF): (W_QKV, 3 * D, 2 * D), ("k", CROSS): (W_KV, 2 * D, 0),
                                   ("v", CROSS): (W_KV, 2 * D, D), ("q", CROSS): (W_Q, D, 0)}[kind, s]
                for part in range(2):
                    for c in range(CT):
                        if kind == "v":
                            cols = slice((2 * half + part) * N, (2 * half + part + 1) * N)
                            lhs, rhs = (hi[:, c, cols], lo[:, c, cols]), w(col, c, stride, at, D)
                        else:
                            cols = slice(half * HALF, (half + 1) * HALF)
                            lhs, rhs = w(col, c, stride, at + part * P, P), (hi[:, c, cols], lo[:, c, cols])
                        mm = product(dst[:, part * HALF:(part + 1) * HALF], lhs, rhs, c == 0, c == CT - 1)
                return mm

            def side_unit(it, step):
                unit, r = SIDE[step]
                if step == -1:
                    y_out(pe, it - 1, 11)
                elif r == P_PROJ:
                    p_proj_free(it, step)
                elif r < 2:
                    pe.wait_ge(exps_made, it * 32 + STEPS - 1 + r)
                else:
                    pe.wait_ge(probs_moved, it * 32 + STEPS - 3 + r)
                make_unit(it, unit, p_proj if r == P_PROJ else ring[r]).then_inc(side_full, 1)

            def p_ln_free(it, z, n):
                uses = sorted([((CROSS_FROM if j >= 4 else 0) + QUADS * (j % 4) + AT_MIX, 0, j) for j in range(8)]
                              + [((CROSS_FROM if j >= 8 else 0) + QUADS * (j % 4) + AT_LNT, 1, j) for j in range(4, 12)])
                at = [u[1:] for u in uses].index((int(z), n))
                if at == 0:
                    pe.wait_ge(ln_moved, it * 12 + 4)
                elif uses[at - 1][1]:
                    pe.wait_ge(ln_moved, it * 12 + uses[at - 1][2] + 1)
                else:
                    pe.wait_ge(rden_moved, it * 8 + uses[at - 1][2] + 1)

            def p_proj_free(it, step, projection=False):
                sides = [t for t in SIDE_STEPS if SIDE[t][1] == P_PROJ]
                uses = sorted([(t, 1, n) for n, t in enumerate(sides)]
                              + [((CROSS_FROM if j >= 4 else 0) + QUADS * (j % 4) + AT_PROJ, 0, j) for j in range(8)])
                at = [n for n, (t, side, _) in enumerate(uses) if t == step and side == (not projection)][0]
                _, side, n = uses[at - 1]
                if side:
                    pe.wait_ge(moved[P_PROJ], it * MOVED[P_PROJ] + n + 1)
                else:
                    y_out(pe, it, n)

            def scores(it, layer, s, g):
                b, q = divmod(g, QUADS)
                if g % (STEPS // 2) == 0:
                    half = g // (STEPS // 2)
                    if layer == 0:
                        moved_by(pe, it, ("k", s, half))
                        moved_by(pe, it, ("q", s, half))
                    else:
                        pe.wait_ge(keys_made, (it - NG) * 4 + 2 * s + half + 1)
                        pe.wait_ge(queries_made, (it - NG) * 4 + 2 * s + half + 1)
                if g == 1 and s == SELF:
                    moved_by(pe, it, ("v", 0, 0))
                if g < 2 and s == CROSS:
                    moved_by(pe, it, IN_BANK[g][-1])
                if g >= 2 or s == CROSS:
                    pe.wait_ge(exps_made, it * 32 + s * STEPS + g - 1)
                dst = ring[g % 2]
                r = slice(32 * q, 32 * q + 32)
                masked = layer == 0 and s == CROSS
                if masked:
                    if g == 0:
                        pe.wait_ge(mask_made, it + 1)
                    rows = mask_row[:, b * N:(b + 1) * N].unsqueeze(1).broadcast_to([P, 4, N])
                    pe.matmul(dst[:].rearrange("p (h n) -> p h n", h=4), ones_row[:], rows,
                              start=True, stop=False, skip_group_check=True)
                for t in range(CT):
                    mm = pe.matmul(dst[:, t * 2 * N:(t + 1) * 2 * N].rearrange("p (e n) -> p e n", e=2),
                                   q_t[r, t, b * N:(b + 1) * N], k_t[s][r, t, :, b * N:(b + 1) * N],
                                   start=not masked, stop=True, skip_group_check=masked)
                mm.then_inc(scored, 1)

            def turn_probs(it, s, g):
                pe.wait_ge(exps_made, it * 32 + s * STEPS + g + 1)
                if g < 2 and s == SELF:
                    moved_by(pe, it, list(FIRST)[g])
                else:
                    if g < 2:
                        moved_by(pe, it, IN_BANK[2 + g][-1])
                    pe.wait_ge(probs_moved, it * 32 + s * STEPS + g - 1)
                for h in range(4):
                    mm = pe.transpose(ring[2 + g % 2][:, h * N:(h + 1) * N], probs[:, (s * STEPS + g) % 3, h, :], ident[:])
                mm.then_inc(probs_turned, 1)

            def mix_values(it, s, b):
                pe.wait_ge(probs_moved, it * 32 + s * STEPS + QUADS * b + QUADS)
                moved_by(pe, it, ("v", s, b // 2))
                if 4 * s + b >= 2:
                    pe.wait_ge(heads_scaled, it * 8 + 4 * s + b - 1)
                elif b == 1:
                    y_out(pe, it - 1, 10)
                dst = mix[b % 2]
                for t in range(CT):
                    for e in range(2):
                        for q in range(QUADS):
                            mm = pe.matmul(dst[32 * q:32 * q + 32, t * N:(t + 1) * N],
                                           v_pad[s][:, b, 8 * t + 2 * q + e, :],
                                           probs_t[:, b % 2, q, 2 * t + e, :],
                                           start=(e == 0), stop=(e == 1), tile_position=(0, 32 * q))
                mm.then_inc(mixed, 1)

            def turn_rden(it, s, b):
                pe.wait_ge(rden_spread, it * 8 + 4 * s + b + 1)
                p_ln_free(it, z=False, n=4 * s + b)
                for t in range(CT):
                    mm = pe.transpose(p_ln[:, t * P:(t + 1) * P], rden_wide[:, t * P:(t + 1) * P], ident[:])
                mm.then_inc(rden_turned, 1)

            def project(it, s, b):
                j = 4 * s + b
                pe.wait_ge(heads_hi_made, it * 8 + j + 1)
                pe.wait_ge(heads_lo_made, it * 8 + j + 1)
                p_proj_free(it, (CROSS_FROM if s else 0) + QUADS * b + AT_PROJ, projection=True)
                for t in range(CT):
                    mm = product(p_proj[:, 0:D], (heads_hi[:, b % 2, t, :], heads_lo[:, b % 2, t, :]),
                                 w(W_SA if s == SELF else W_CA, t, D, 0, D), t == 0, t == CT - 1)
                mm.then_inc(projected, 1)

            def up(it, u):
                if u == 2:
                    pe.wait_ge(probs_moved, it * 32 + 32)
                if u >= MLP_RING:
                    up_moved(pe, it, u - MLP_RING)
                half, f = divmod(u, FT)
                if f == 0:
                    pe.wait_ge(xt_hi_made, it * 12 + 8 + 2 * half + 2)
                    pe.wait_ge(xt_lo_made, it * 12 + 8 + 2 * half + 2)
                cols = slice(half * HALF, (half + 1) * HALF)
                for c in range(CT):
                    mm = product(ring[u % MLP_RING][:, 0:HALF], w(W_F1, c, DF, f * P, P),
                                 (xt_hi[:, c, cols], xt_lo[:, c, cols]), c == 0, c == CT - 1)
                mm.then_inc(up_full, 1)

            def down(it, u):
                half, f = divmod(u, FT)
                pe.wait_ge(hid_hi_made, it * HIDDEN + u + 1)
                pe.wait_ge(hid_lo_made, it * HIDDEN + u + 1)
                if f == 0:
                    pe.wait_ge(heads_scaled, it * 8 + (7 if half == 0 else 8))
                    if half == 0:
                        pe.wait_ge(probs_moved, it * 32 + 32)
                    else:
                        y_out(pe, it, 7)
                slot = u % HID_SLOTS
                for k in range(2):
                    mm = product(y_mlp[2 * half + k][:, 0:D],
                                 (hid_hi[:, slot, k * N:(k + 1) * N], hid_lo[:, slot, k * N:(k + 1) * N]),
                                 w(W_F2, f, D, 0, D), f == 0, f == FT - 1)
                    if f == FT - 1 and k == 0:
                        mm.then_inc(fc2_full, 1)
                if f == FT - 1:
                    mm.then_inc(fc2_full, 1)
                else:
                    mm.then_inc(hid_used, 1)

            def mlp(it, kind, u):
                (up if kind == "up" else down)(it, u)

            def attention(it, layer):
                for step in range(LAST_STEP + 1):
                    for s, g in quad_at(step, 0):
                        scores(it, layer, s, g)
                    for s, g in quad_at(step, AT_TURN):
                        turn_probs(it, s, g)
                    for s, b in batch_at(step, AT_MIX):
                        turn_rden(it, s, b)
                        mix_values(it, s, b)
                    for s, b in batch_at(step, AT_PROJ):
                        project(it, s, b)
                    for s, b in batch_at(step, AT_LNT):
                        turn_z(it, s + 1, b)
                    if step in SIDE:
                        side_unit(it, step)
                    for unit in FIRST_HALF.get(step, ()):
                        mlp(it, *unit)

            pe.wait_ge(c_loaded, 16 * (CONST_LOADS - 1))
            pe.wait_ge(silu_step, 4)
            ada = stage[:, 0:CT * 6 * D].rearrange("p (t n) -> p t n", t=CT)
            lnw = [k_t[0][:].rearrange("p t e n -> p (t e n)").rearrange("p (m t n) -> p m t n", m=2, t=CT)[:, m]
                   for m in range(2)] + [q_t[:]]
            n = 0
            for chunk in (1, 0, 4, 3):
                for o in range(CT):
                    for c in range(CT):
                        mm = pe.matmul(mix[0][:, n * B:(n + 1) * B],
                                       ada[:, c, chunk * D + o * P:chunk * D + (o + 1) * P], silu[:, c, :],
                                       start=(c == 0), stop=(c == CT - 1))
                    n += 1
            for g, chunk in enumerate((2, 5)):
                for c in range(CT):
                    mm = pe.matmul(p_proj[0:B, g * D:(g + 1) * D], silu[:, c, :],
                                   ada[:, c, chunk * D:(chunk + 1) * D], start=(c == 0), stop=(c == CT - 1))
            mm.then_inc(mod_full, 1)
            n = 0
            for k in range(3):
                for half in range(2):
                    for o in range(CT):
                        for c in range(CT):
                            mm = pe.matmul(mix[1][:, n * B:(n + 1) * B],
                                           lnw[k][:, c, half * D + o * P:half * D + (o + 1) * P], cond[:, c, :],
                                           start=(c == 0), stop=(c == CT - 1))
                        n += 1
            mm.then_inc(mod_full, 1)

            for b in range(GB):
                turn_z(0, 0, b)
            for layer in range(LAYERS):
                pe.wait_ge(w_hi_made, 4 * layer + 4)
                pe.wait_ge(w_lo_made, 4 * layer + 4)
                with pe.Fori(0, NG) as i:
                    it = i + layer * NG
                    for unit, r in FIRST.items():
                        make_unit(it, unit, ring[r]).then_inc(first_full, 1)
                    side_unit(it, -1)
                    attention(it, layer)
                    for kind, u in mlp_order(1):
                        mlp(it, kind, u)
                        for b in {("up", 11): (0,), ("down", 8): (1,), ("up", 15): (2,), ("down", 13): (3,)}.get((kind, u), ()):
                            turn_z(it + 1, 0, b)

        @block.scalar
        def _(act):
            def modulate(it, k, b):
                act.wait_ge(z_turned, it * 12 + 4 * k + b + 1)
                if not (isinstance(it, int) and b < 2):
                    act.wait_ge(xt_lo_made, it * 12 + 4 * k + b - 1)
                if k == 0 and b == 0:
                    act.wait_ge(first_copied, it + 1)
                if k == 1 and b == 0:
                    act.wait_ge(mod_copied, it + 1)
                for c in range(CT):
                    table, m = (mod_first, 0) if k == 0 else (mod_now, 4 * (k - 1))
                    op = act.activation(xt[:, b % 2, c, :], p_ln[:, c * P:(c + 1) * P], ACT.Identity,
                                        scale=table[:, m + c, b:b + 1], bias=table[:, m + 2 + c, b:b + 1])
                op.then_inc(ln_moved, 1)
                act.wait_ge(ln_moved, it * 12 + 4 * k + b + 1)
                act.copy(xt_hi[:, :, b * N:(b + 1) * N], xt[:, b % 2, :, :]).then_inc(xt_hi_made, 1)

            def move_unit(it, layer, unit, src, signal):
                kind, s, half = unit
                m = 2 * s + half
                if layer == 0 and kind == "q":
                    for t in range(CT):
                        op = act.activation(q_t[:, t, half * HALF:(half + 1) * HALF], src[:, t * HALF:(t + 1) * HALF],
                                            ACT.Identity, scale=SCALE,
                                            bias=bias_cols[:, 4 + 2 * s + t:5 + 2 * s + t])
                    op.then_inc(signal, 1)
                elif layer == 0:
                    for t in range(CT):
                        for e in range(2):
                            op = act.activation(k_t[s][:, t, e, half * HALF:(half + 1) * HALF],
                                                src[:, t * HALF:(t + 1) * HALF], ACT.Identity,
                                                scale=head_mask[:, e:e + 1], bias=bias_masked[:, e, t:t + 1])
                    op.then_inc(signal, 1)
                else:
                    if m:
                        act.wait_ge(queries_made if kind == "q" else keys_summed, (it - NG) * 4 + m)
                    act.activation(raw[:, int(kind == "q"), :], src[:], ACT.Copy, scale=SCALE if kind == "q" else 1.0)\
                       .then_inc(signal, 1)

            def move_first(it, layer, n):
                unit, r = list(FIRST.items())[n]
                if unit[0] == "q" or (layer == 1 and unit[0] == "k"):
                    act.wait_ge(first_full, it * len(FIRST) + n + 1)
                    move_unit(it, layer, unit, ring[r], moved[r])

            def move_side(it, layer, step):
                unit, r = SIDE[step]
                if unit[0] == "q" or unit == ACT_KEYS or (layer == 1 and unit[0] == "k"):
                    act.wait_ge(side_full, it * len(SIDE) + SIDE_STEPS.index(step) + 1)
                    move_unit(it, layer, unit, (ring + [p_proj])[r], moved[r])

            def gelu(it, layer, u):
                act.wait_ge(up_full, it * HIDDEN + u + 1)
                if u >= 2:
                    act.wait_ge(hid_lo_made, it * HIDDEN + u - 1)
                m = 8 + FT * layer + u % FT
                act.activation(hid[:, u % 2, :], ring[u % MLP_RING][:, 0:HALF], ACT.Gelu, bias=bias_cols[:, m:m + 1])\
                   .then_inc(moved[u % MLP_RING], 1)

            def exps(it, s, g):
                b, q = divmod(g, QUADS)
                act.wait_ge(max_made, it * 32 + s * STEPS + g + 1)
                G = s * STEPS + g
                if G >= 3:
                    act.wait_ge(probs_turned, it * 32 + G - 2)
                for h in range(4):
                    head = 8 * (h // 2) + 2 * q + h % 2
                    op = act.activation(probs[:, G % 3, h, :], ring[g % 2][:, h * N:(h + 1) * N], ACT.Exp,
                                        bias=neg_max[:, g % 2, h:h + 1], accum_out=row_sum[:, b % 2, head:head + 1])
                op.then_inc(exps_made, 1)

            def move_rden(it, s, b):
                act.wait_ge(rden_turned, it * 8 + 4 * s + b + 1)
                act.copy(rden_t[:], p_ln[:, 0:D]).then_inc(rden_moved, 1)

            def split_heads(it, s, b):
                act.wait_ge(heads_scaled, it * 8 + 4 * s + b + 1)
                act.copy(heads_hi[:, b % 2], heads[:, b % 2]).then_inc(heads_hi_made, 1)

            def attention(it, layer):
                for step in range(LAST_STEP + 1):
                    for s, g in quad_at(step, 0):
                        exps(it, s, g)
                    for s, b in batch_at(step, AT_MIX):
                        move_rden(it, s, b)
                    for s, b in batch_at(step, AT_SCALE):
                        split_heads(it, s, b)
                    for s, b in batch_at(step, AT_LNT):
                        modulate(it, s + 1, b)
                    if step in SIDE:
                        move_side(it, layer, step)
                    if step == AT_CTX:
                        act.wait_ge(ctx_loaded, (it + 1) * 16)
                        act.copy(ctx_hi[:], ctxt[:]).then_inc(ctx_hi_made, 1)
                    for kind, u in FIRST_HALF.get(step, ()):
                        if kind == "up":
                            gelu(it, layer, u)

            act.wait_ge(c_loaded, 16 * (CONST_LOADS - 1))
            act.activation(silu_tmp[:], cond[:], ACT.Exp, scale=-1.0).then_inc(silu_step, 1)
            def split_weights(layer):
                for c in range(4):
                    n = 4 * layer + c
                    act.wait_ge(w_loaded[c % 2], 16 * W_LOADS[n])
                    act.copy(w_hi[:, c * CHUNK:(c + 1) * CHUNK], stage[:, (c % 2) * CHUNK:(c % 2 + 1) * CHUNK])\
                       .then_inc(w_hi_made, 1)

            split_weights(0)
            for b in range(GB):
                modulate(0, 0, b)
            for layer in range(LAYERS):
                if layer:
                    split_weights(1)
                with act.Fori(0, NG) as i:
                    it = i + layer * NG
                    for n in range(len(FIRST)):
                        move_first(it, layer, n)
                    move_side(it, layer, -1)
                    attention(it, layer)
                    for kind, u in mlp_order(1):
                        if kind == "up":
                            gelu(it, layer, u)
                            for b in {10: (0,), 11: (1,), 15: (2, 3)}.get(u, ()):
                                modulate(it + 1, 0, b)

        @block.vector
        def _(dve):
            def moments(it, layer, k, b):
                j = 4 * k + b
                if k == 0:
                    dve.wait_ge(x_loaded, (it + 1) * 16)
                else:
                    x_ready(dve, layer, it - layer * NG, j - 4)
                src = x_new if k == 0 else x
                dve.bn_stats(stats[:, b, :], src[:, b, :]).then_inc(stats_made, 1)
                dve.wait_ge(stats_made, it * 12 + j + 1)
                dve.sem_inc(dve_held, 1)
                dve.bn_aggr(mean_var[:, b, :], stats[:, b, :]).then_inc(moments_made, 1)

            def normalise(it, k, b):
                dve.wait_ge(rstd_made, it * 12 + 4 * k + b + 1)
                src = x_new if k == 0 else x
                dve.tensor_scalar(z[:, b, :], src[:, b, :], mean_var[:, b, 0:1], rstd[:, b:b + 1],
                                  ALU.subtract, ALU.mult).then_inc(z_made, 1)

            def put_values(layer, s, b, src):
                for e in range(2):
                    dst = v_pad[s][:, b].rearrange("p h w -> p (h w)").rearrange("p (a e w) -> p a e w", a=H // 2, e=2)\
                        [:, :, e, e * HD:(e + 1) * HD]
                    heads_of = src.rearrange("p (a e d) -> p a e d", a=H // 2, e=2)[:, :, e, :]
                    if layer == 0:
                        bias = bias_rows[:, s, :].rearrange("p (a e d) -> p a e d", a=H // 2, e=2)[:, :, e, :]
                        op = dve.tensor_tensor(dst, heads_of, bias, ALU.add)
                    else:
                        op = dve.tensor_copy(dst, heads_of)
                return op

            def put_keys(s, half, src):
                for t in range(CT):
                    for e in range(2):
                        op = dve.tensor_scalar(k_t[s][:, t, e, half * HALF:(half + 1) * HALF],
                                               src[:, t * HALF:(t + 1) * HALF],
                                               bias_cols[:, 2 * s + t:2 * s + t + 1],
                                               head_mask[:, e:e + 1], ALU.add, ALU.mult)
                return op

            def swap(it, unit):
                g, n, which = it - NG, ROPED.index(unit), int(unit[0] == "q")
                moved_by(dve, it, unit)
                dve.sem_inc(dve_held, 1)
                dve.stream_shuffle(rot[:, which, :], raw[:, which, :], SWAP).then_inc(swapped, 1)
                if unit in FIRST or unit[0] == "q":
                    dve.wait_ge(swapped, g * len(ROPED) + n + 1)
                    table = sin_t[:].unsqueeze(1).broadcast_to([P, GB, N])
                    rot3 = rot[:, which, :].rearrange("p (b n) -> p b n", b=GB)
                    dve.tensor_tensor(rot3, rot3, table, ALU.mult).then_inc(sin_made, 1)

            def mask_keys(it, unit):
                _, s, half = unit
                g = it - NG
                if unit in FIRST:
                    dve.wait_ge(sin_made, g * 5 + 2)
                    dve.wait_ge(cos_made, g * len(ROPED) + ROPED.index(unit) + 1)
                    dve.tensor_tensor(rot[:, 0, :], raw[:, 0, :], rot[:, 0, :], ALU.add).then_inc(keys_summed, 1)
                dve.wait_ge(keys_summed, g * 4 + 2 * s + half + 1)
                for e in range(2):
                    op = dve.tensor_scalar(k_t[s][:, :, e, half * HALF:(half + 1) * HALF],
                                           rot[:, 0, :].rearrange("p (t n) -> p t n", t=CT),
                                           head_mask[:, e:e + 1], None, ALU.mult)
                op.then_inc(keys_made, 1)

            def move_unit(it, layer, unit, src):
                kind, s, half = unit
                if kind == "k":
                    return put_keys(s, half, src)
                for k in range(2):
                    op = put_values(layer, s, 2 * half + k, src[:, k * D:(k + 1) * D])
                return op

            def move_first(it, layer, n):
                unit, r = list(FIRST.items())[n]
                if layer == 1 and unit[0] != "v":
                    swap(it, unit)
                    if unit[0] == "k":
                        mask_keys(it, unit)
                elif unit[0] != "q":
                    dve.wait_ge(first_full, it * len(FIRST) + n + 1)
                    move_unit(it, layer, unit, ring[r]).then_inc(moved[r], 1)

            def move_side(it, layer, step):
                unit, r = SIDE[step]
                if unit[0] == "v" or (unit[0] == "k" and unit != ACT_KEYS and layer == 0):
                    dve.wait_ge(side_full, it * len(SIDE) + SIDE_STEPS.index(step) + 1)
                    move_unit(it, layer, unit, (ring + [p_proj])[r]).then_inc(moved[r], 1)

            def row_max(it, s, g):
                dve.wait_ge(scored, it * 32 + s * STEPS + g + 1)
                dve.tensor_reduce(neg_max[:, g % 2, :], ring[g % 2][:].rearrange("p (h n) -> p h n", h=4),
                                  AX.X, ALU.max, negate=True).then_inc(max_made, 1)

            def move_probs(it, s, g):
                b, q = divmod(g, QUADS)
                dve.wait_ge(probs_turned, it * 32 + s * STEPS + g + 1)
                dve.tensor_copy(probs_t[:, b % 2, q].rearrange("p h n -> p (h n)"), ring[2 + g % 2][:])\
                   .then_inc(probs_moved, 1)

            def make_rden(it, s, b):
                j = 4 * s + b
                dve.wait_ge(exps_made, it * 32 + s * STEPS + QUADS * b + QUADS)
                dve.reciprocal(rden[:, b % 2, :], row_sum[:, b % 2, :]).then_inc(rden_made, 1)
                dve.wait_ge(rden_made, it * 8 + j + 1)
                dve.tensor_copy(rden_wide[:].rearrange("p (h d) -> p h d", h=H),
                                rden[:, b % 2, :].unsqueeze(2).broadcast_to([P, H, HD])).then_inc(rden_spread, 1)

            def scale_heads(it, s, b):
                j = 4 * s + b
                dve.wait_ge(mixed, it * 8 + j + 1)
                dve.wait_ge(rden_moved, it * 8 + j + 1)
                dve.tensor_tensor(heads[:, b % 2].rearrange("p t n -> p (t n)"), mix[b % 2][:, 0:D], rden_t[:],
                                  ALU.mult).then_inc(heads_scaled, 1)

            def take_output(it, layer, j):
                b = j % 4
                if j < 8:
                    dve.wait_ge(projected, it * 8 + j + 1)
                    src = p_proj[:, 0:D]
                else:
                    dve.wait_ge(fc2_full, it * 4 + b + 1)
                    src = y_mlp[b][:, 0:D]
                if layer == 1 and j < 8:
                    if j == 0:
                        dve.wait_ge(stored, it * 16 + 16 * GATE_STORES)
                    dve.tensor_tensor(x[:, b, :], src, x_new[:, b, :] if j < 4 else x[:, b, :], ALU.add)\
                       .then_inc(y_moved, 1)
                else:
                    if j >= 2:
                        if layer == 0:
                            dve.wait_ge(x_updated, it * 12 + j - 1)
                        elif j >= 10:
                            dve.wait_ge(x_updated, (it - NG) * 4 + 12 * NG + j - 9)
                    row = 2 + j // 4 if layer == 0 else 5
                    dve.tensor_tensor(delta[:, j % 2, :], src, bias_rows[:, row, :], ALU.add).then_inc(y_moved, 1)

            def hi_hidden(it, u):
                up_moved(dve, it, u)
                if u >= HID_SLOTS:
                    dve.wait_ge(*slot_free(it, u - HID_SLOTS))
                dve.tensor_copy(hid_hi[:, u % HID_SLOTS, :], hid[:, u % 2, :]).then_inc(hid_hi_made, 1)

            def slot_free(it, u):
                half, f = divmod(u, FT)
                if f == FT - 1:
                    return fc2_full, it * 4 + 2 * half + 2
                return hid_used, it * (HIDDEN - 2) + u - half + 1

            def attention(it, layer):
                for step in range(LAST_STEP + 1):
                    for s, g in quad_at(step, 0):
                        row_max(it, s, g)
                    if layer == 0 and step == AT_MASK:
                        dve.wait_ge(side_loaded, (it + 1) * 32)
                        dve.tensor_scalar(mask_row[:], mask_u8[:], MASKED / P, None, ALU.mult).then_inc(mask_made, 1)
                    for s, g in quad_at(step, AT_TURN):
                        move_probs(it, s, g)
                    for s, b in batch_at(step, AT_RDEN):
                        make_rden(it, s, b)
                    for s, b in batch_at(step, AT_SCALE):
                        scale_heads(it, s, b)
                    for s, b in batch_at(step, AT_PROJ):
                        take_output(it, layer, 4 * s + b)
                    for s, b in batch_at(step, AT_STATS):
                        moments(it, layer, s + 1, b)
                    for s, b in batch_at(step, AT_Z):
                        normalise(it, s + 1, b)
                    if step in SIDE:
                        move_side(it, layer, step)
                    if layer == 1:
                        for unit in roped_at(step, SWAP_LAG):
                            swap(it, unit)
                        for unit in roped_at(step, MASK_LAG):
                            if unit[0] == "k":
                                mask_keys(it, unit)
                    for kind, u in FIRST_HALF.get(step, ()):
                        if kind == "up":
                            hi_hidden(it, u)

            dve.memset(ones_row[:], 1.0).then_inc(ready, 1)
            for s in range(2):
                dve.memset(v_pad[s][:], 0.0).then_inc(ready, 1)
            dve.memset(mod[:, 5:7, 0:B], 1.0).then_inc(ready, 1)
            dve.memset(mod[:, 7:9, 0:B], 0.0).then_inc(ready, 1)
            dve.memset(mod[:, :, LAYERS * B:], 1.0).then_inc(ready, 1)
            for layer in range(LAYERS):
                dve.memset(eps_cols[:, layer:layer + 1], EPS[layer]).then_inc(ready, 1)
                dve.memset(mod[:, 4, layer * B:(layer + 1) * B], EPS[layer]).then_inc(ready, 1)
            dve.wait_ge(silu_step, 1)
            dve.tensor_scalar(silu_tmp[:], silu_tmp[:], 1.0, None, ALU.add).then_inc(silu_step, 1)
            dve.wait_ge(silu_step, 2)
            dve.reciprocal(silu_tmp[:], silu_tmp[:]).then_inc(silu_step, 1)
            dve.wait_ge(silu_step, 3)
            dve.tensor_tensor(silu[:], cond[:], silu_tmp[:], ALU.mult).then_inc(silu_step, 1)
            dve.tensor_scalar(bias_cols[:, 4:8], bias_cols[:, 4:8], SCALE, None, ALU.mult).then_inc(ready, 1)
            for e in range(2):
                dve.tensor_scalar(bias_masked[:, e, :], bias_cols[:, 0:CT], head_mask[:, e:e + 1], None, ALU.mult)\
                   .then_inc(ready, 1)
            dve.wait_ge(mod_full, 1)
            def put_mod(layer, k, src, bias):
                row = 0 if k == 0 else 1 + 4 * k
                dve.tensor_tensor(mod[:, row:row + 4, layer * B:(layer + 1) * B],
                                  src.rearrange("p (m b) -> p m b", m=4),
                                  bias.unsqueeze(2).broadcast_to([P, 4, B]), ALU.add).then_inc(mod_step, 1)

            for m, k in enumerate((0, 2)):
                put_mod(0, k, mix[0][:, m * 4 * B:(m + 1) * 4 * B], bias_mod[:, 4 * m:4 * m + 4])
            dve.tensor_tensor(raw[0:B, 1, :], p_proj[0:B, :],
                              raw[0:B, 0, :], ALU.add).then_inc(y_moved, 1)
            dve.wait_ge(mod_full, 2)
            for k in range(3):
                put_mod(1, k, mix[1][:, k * 4 * B:(k + 1) * 4 * B], bias_mod[:, 8 + 4 * k:12 + 4 * k])
            dve.wait_ge(mod_step, 5)
            for layer, k in ((0, 0), (0, 2), (1, 0), (1, 1), (1, 2)):
                row = 0 if k == 0 else 1 + 4 * k
                scales = mod[:, row:row + 2, layer * B:(layer + 1) * B]
                dve.tensor_scalar(scales, scales, 1.0, None, ALU.add).then_inc(mod_step, 1)
            dve.wait_ge(mod_step, 10)
            dve.wait_ge(ready, 13)
            dve.tensor_copy(mod_first[:], mod[:, 0:5, 0:GB]).then_inc(first_copied, 1)
            for b in range(GB):
                moments(0, 0, 0, b)
            for b in range(GB):
                normalise(0, 0, b)

            tail = ("m0 m1 z0 z1 h8 o8 h9 o9 m2 h10 m3 h11 z2 z3 h12 h13 h14 h15 o10 o11").split()
            for layer in range(LAYERS):
                for c in range(4):
                    n = 4 * layer + c
                    dve.wait_ge(w_hi_made, n + 1)
                    dve.tensor_tensor(w_lo[:, c * CHUNK:(c + 1) * CHUNK], stage[:, (c % 2) * CHUNK:(c % 2 + 1) * CHUNK],
                                      w_hi[:, c * CHUNK:(c + 1) * CHUNK].bitcast(F32), ALU.subtract).then_inc(w_lo_made, 1)
                with dve.Fori(0, NG) as i:
                    it = i + layer * NG
                    dve.tensor_copy(mod_now[:], mod[:, 5:13, bass.ds(i * GB + layer * B, GB)]).then_inc(mod_copied, 1)
                    for n in range(len(FIRST)):
                        move_first(it, layer, n)
                    move_side(it, layer, -1)
                    attention(it, layer)
                    dve.tensor_copy(mod_first[:], mod[:, 0:5, bass.ds(i * GB + (layer * B + GB), GB)])\
                       .then_inc(first_copied, 1)
                    for what in tail:
                        n = int(what[1:])
                        if what[0] == "h":
                            hi_hidden(it, n)
                        elif what[0] == "o":
                            take_output(it, layer, n)
                        elif what[0] == "m":
                            moments(it + 1, layer, 0, n)
                        else:
                            normalise(it + 1, 0, n)

        @block.gpsimd
        def _(pool):
            def make_rstd(it, layer, k, b):
                j = 4 * k + b
                pool.wait_ge(moments_made, it * 12 + j + 1)
                if k == 0 and b == 0:
                    pool.wait_ge(first_copied, it + 1)
                eps = mod_first[:, 4, 0:1] if k == 0 else eps_cols[:, layer:layer + 1]
                pool.tensor_tensor(var_eps[:, b:b + 1], mean_var[:, b, 1:2], eps, ALU.add).then_inc(eps_added, 1)
                pool.wait_ge(eps_added, it * 12 + j + 1)
                pool.tensor_tensor(rstd[:, b:b + 1], var_eps[:, b:b + 1], minus_half[:], ALU.pow).then_inc(rstd_made, 1)

            def split_xt(it, k, b):
                pool.wait_ge(xt_hi_made, it * 12 + 4 * k + b + 1)
                cols = slice(b * N, (b + 1) * N)
                pool.tensor_tensor(xt_lo[:, :, cols], xt[:, b % 2], xt_hi[:, :, cols].bitcast(F32), ALU.subtract)\
                    .then_inc(xt_lo_made, 1)

            def split_heads(it, s, b):
                pool.wait_ge(heads_hi_made, it * 8 + 4 * s + b + 1)
                pool.tensor_tensor(heads_lo[:, b % 2], heads[:, b % 2], heads_hi[:, b % 2].bitcast(F32), ALU.subtract)\
                    .then_inc(heads_lo_made, 1)

            def add_output(it, layer, j):
                b = j % 4
                if layer == 1 and j < 8:
                    return
                y_out(pool, it, j)
                if layer == 0 and not 4 <= j < 8:
                    g = j // 8
                    if j == 0:
                        pool.wait_ge(side_loaded, (it + 1) * 32)
                    pool.tensor_tensor(delta[:, j % 2, :], delta[:, j % 2, :], gate_now[:, b, g, :], ALU.mult)\
                        .then_inc(gated, 1)
                    pool.wait_ge(gated, it * 8 + (j if j < 4 else j - 4) + 1)
                if j == 0:
                    pool.wait_ge(stored, it * 16 + 16 * GATE_STORES)
                pool.tensor_tensor(x[:, b, :], x_new[:, b, :] if j < 4 else x[:, b, :], delta[:, j % 2, :], ALU.add)\
                    .then_inc(x_updated, 1)

            def times_cos(it, unit):
                n, which = ROPED.index(unit), int(unit[0] == "q")
                pool.wait_ge(swapped, (it - NG) * len(ROPED) + n + 1)
                blocks = lambda v: v[:, which, :].rearrange("p (b n) -> p b n", b=GB)
                pool.tensor_tensor(blocks(raw), blocks(raw), cos_t[:].unsqueeze(1).broadcast_to([P, GB, N]), ALU.mult)\
                    .then_inc(cos_made, 1)

            def finish_rotation(it, unit):
                kind, s, half = unit
                g, n = it - NG, ROPED.index(unit)
                blocks = lambda v: v[:, 0, :].rearrange("p (b n) -> p b n", b=GB)
                if kind == "q":
                    pool.wait_ge(cos_made, g * len(ROPED) + n + 1)
                    pool.wait_ge(sin_made, g * 5 + (1 if unit in FIRST else 2 + 2 * s + half))
                    pool.tensor_tensor(q_t[:, :, half * HALF:(half + 1) * HALF],
                                       raw[:, 1, :].rearrange("p (t n) -> p t n", t=CT),
                                       rot[:, 1, :].rearrange("p (t n) -> p t n", t=CT), ALU.add).then_inc(queries_made, 1)
                elif unit not in FIRST:
                    pool.tensor_tensor(blocks(rot), blocks(rot), sin_t[:].unsqueeze(1).broadcast_to([P, GB, N]), ALU.mult)\
                        .then_inc(sin_keys, 1)
                    pool.wait_ge(cos_made, g * len(ROPED) + n + 1)
                    pool.wait_ge(sin_keys, g * 3 + 2 * s + half)
                    pool.tensor_tensor(rot[:, 0, :], raw[:, 0, :], rot[:, 0, :], ALU.add).then_inc(keys_summed, 1)

            def lo_hidden(it, u):
                pool.wait_ge(hid_hi_made, it * HIDDEN + u + 1)
                pool.tensor_tensor(hid_lo[:, u % HID_SLOTS, :], hid[:, u % 2, :],
                                   hid_hi[:, u % HID_SLOTS, :].bitcast(F32), ALU.subtract).then_inc(hid_lo_made, 1)

            def attention(it, layer):
                for step in range(LAST_STEP + 1):
                    for s, b in batch_at(step, AT_SCALE):
                        split_heads(it, s, b)
                    for s, b in batch_at(step, AT_PROJ):
                        add_output(it, layer, 4 * s + b)
                    for s, b in batch_at(step, AT_STATS):
                        make_rstd(it, layer, s + 1, b)
                    for s, b in batch_at(step, AT_LNT):
                        split_xt(it, s + 1, b)
                    for unit in roped_at(step, SWAP_LAG) if layer == 1 else ():
                        times_cos(it, unit)
                        finish_rotation(it, unit)
                    if step == AT_CTX:
                        pool.wait_ge(ctx_hi_made, it + 1)
                        pool.tensor_tensor(ctx_lo[:], ctxt[:], ctx_hi[:].bitcast(F32), ALU.subtract).then_inc(ctx_lo_made, 1)
                    for kind, u in FIRST_HALF.get(step, ()):
                        if kind == "up":
                            lo_hidden(it, u)

            pool.memset(minus_half[:], -0.5).then_inc(half_made, 1)
            pool.wait_ge(half_made, 1)
            for b in range(GB):
                make_rstd(0, 0, 0, b)
            for b in range(GB):
                split_xt(0, 0, b)
            tail = ("r0 r1 l8 l9 r2 o8 l10 x0 r3 l11 x1 o9 l12 l13 l14 l15 x2 x3 o10 o11").split()
            for layer in range(LAYERS):
                with pool.Fori(0, NG) as i:
                    it = i + layer * NG
                    if layer == 1:
                        times_cos(it, ("q", 0, 0))
                        times_cos(it, ("k", 0, 0))
                        finish_rotation(it, ("q", 0, 0))
                    attention(it, layer)
                    for what in tail:
                        n = int(what[1:])
                        if what[0] == "l":
                            lo_hidden(it, n)
                        elif what[0] == "o":
                            add_output(it, layer, n)
                        elif what[0] == "r":
                            make_rstd(it + 1, layer, 0, n)
                        else:
                            split_xt(it + 1, 0, n)


SWAP = [16 * (p // 16) + (p % 16 + HD // 2) % HD for p in range(32)]

WEIGHTS = [
    [[("L0_xcond_qkv_w", W_QKV, CT, 3 * D), ("L0_xcond_sa_proj_w", W_SA, CT, D)],
     [("L0_xcond_q_w", W_Q, CT, D), ("L0_xcond_kv_w", W_KV, CT, 2 * D), ("L0_xcond_ca_proj_w", W_CA, CT, D)],
     [("L0_xcond_fc1_w", W_F1, CT, DF)],
     [("L0_xcond_fc2_w", W_F2, FT, D)]],
    [[("L1_qkv_wT", W_QKV, CT, 3 * D), ("L1_sa_wT", W_SA, CT, D)],
     [("L1_q_wT", W_Q, CT, D), ("L1_kv_wT", W_KV, CT, 2 * D), ("L1_ca_wT", W_CA, CT, D)],
     [("L1_f1_wT", W_F1, CT, DF)],
     [("L1_f2_wT", W_F2, FT, D)]],
]
_PARTS = [len(c) for layer in WEIGHTS for c in layer]
W_LOADS = [sum(_PARTS[n % 2:n + 1:2]) for n in range(len(_PARTS))]


def rope_tables():
    half = HD // 2
    inv = (1.0 / np.float32(10000.0) ** (np.arange(half, dtype=np.float32) / np.float32(half))).astype(np.float32)
    ang = np.arange(N, dtype=np.float32)[None, :] * inv[:, None]
    cos, sin = np.cos(ang), np.sin(ang)
    return np.tile(cos, (P // half, 1)), np.tile(np.concatenate([-sin, sin]), (P // HD, 1))


def kernel(**inputs):
    import concourse.bacc as bacc
    from concourse.bass_utils import run_bass_kernel_spmd as run

    get = {k: np.asarray(v) for k, v in inputs.items()}
    cols = lambda v: v.reshape(-1, P).T
    zeros = np.zeros
    ada_b = get["L0_xcond_ada_b"].reshape(6, D)
    qkv_b = get["L0_xcond_qkv_b"].reshape(3, D)
    kv_b = get["L0_xcond_kv_b"].reshape(2, D)
    cos, sin = rope_tables()
    arrays = {
        "x": get["x"].reshape(B * N, D),
        "condT": get["cond_1024"].T,
        "ctxT": get["ctx_1024"].reshape(B * N, D).T,
        "mask": get["mask_BxS2_bf0"].reshape(B * N).view(np.uint32),
        "L0_xcond_ada_w": get["L0_xcond_ada_w"],
        "ln_wT": np.stack([get[f"L1_xcond_ln{k}_w"].T for k in (1, 2, 3)]),
        "bias_mod": np.concatenate([cols(ada_b[c]) for c in (1, 0, 4, 3)]
                                   + [cols(get[f"L1_xcond_ln{k}_b"]) for k in (1, 2, 3)], axis=1),
        "gate_bias": np.stack([ada_b[2], ada_b[5]]),
        "ident": np.eye(P, dtype=np.float32),
        "head_mask": np.stack([np.arange(P) % 32 < HD, np.arange(P) % 32 >= HD], axis=1).astype(np.float32),
        "cos_t": cos,
        "sin_t": sin,
        "bias_rows": np.stack([qkv_b[2], kv_b[1], get["L0_xcond_sa_proj_b"], get["L0_xcond_ca_proj_b"],
                               get["L0_xcond_fc2_b"], get["L1_xcond_ffn_b2"]]),
        "bias_cols": np.concatenate([cols(qkv_b[1]), cols(kv_b[0]), cols(qkv_b[0]), cols(get["L0_xcond_q_b"]),
                                     cols(get["L0_xcond_fc1_b"]), cols(get["L1_xcond_ffn_b1"])], axis=1),
        "L1_qkv_wT": get["L1_xcond_qkv_w"].T,
        "L1_sa_wT": get["L1_xcond_sa_out_w"].T,
        "L1_q_wT": get["L1_xcond_q_w"].T,
        "L1_kv_wT": np.concatenate([get["L1_xcond_k_w"].T, get["L1_xcond_v_w"].T], axis=1),
        "L1_ca_wT": get["L1_xcond_ca_out_w"].T,
        "L1_f1_wT": get["L1_xcond_ffn_w1"].T,
        "L1_f2_wT": get["L1_xcond_ffn_w2"].T,
    }
    for name in ("qkv", "sa_proj", "q", "kv", "ca_proj", "fc1", "fc2"):
        arrays[f"L0_xcond_{name}_w"] = get[f"L0_xcond_{name}_w"]
    arrays = {k: np.ascontiguousarray(v) for k, v in arrays.items()}

    nc = bacc.Bacc("TRN2", target_bir_lowering=False, num_devices=1)
    a = {k: nc.dram_tensor(f"in_{k}", v.shape, mybir.dt.from_np(v.dtype), kind="ExternalInput").ap()
         for k, v in arrays.items()}
    x_mid = nc.dram_tensor("x_mid", (B * N, D), F32, kind="Internal").ap()
    gates = nc.dram_tensor("gates", (B, 2, D), F32, kind="Internal").ap()
    out = nc.dram_tensor("out", (B * N, D), F32, kind="ExternalOutput").ap()
    build_blocks(nc, a, x_mid, gates, out)
    r = run(nc, [{f"in_{k}": v for k, v in arrays.items()}], core_ids=[0])
    return r.results[0]["out"].reshape(B, N, D)
```

```python
from contextlib import ExitStack

import numpy as np
import concourse.bass as bass
from concourse import mybir

F32 = mybir.dt.float32
F32R = mybir.dt.float32r
BF16 = mybir.dt.bfloat16
U8 = mybir.dt.uint8
U32 = mybir.dt.uint32
ALU = mybir.AluOpType
ACT = mybir.ActivationFunctionType
AX = mybir.AxisListType

P = 128
B, N, D, H = 32, 128, 256, 16
HD = D // H
DF = 4 * D
CT = D // P
FT = DF // P
GB = 4
NG = B // GB
GN = GB * N
LAYERS = 2
EPS = (1e-6, 1e-5)
SCALE = HD ** -0.5
MASKED = -1e30
COPIES = 4
QUADS = 4
STEPS = GB * QUADS
SELF, CROSS = 0, 1

W_QKV = 0
W_SA = W_QKV + CT * 3 * D
W_Q = W_SA + CT * D
W_KV = W_Q + CT * D
W_CA = W_KV + CT * 2 * D
W_F1 = W_CA + CT * D
W_F2 = W_F1 + CT * DF
W_ALL = W_F2 + FT * D
CHUNK = W_ALL // 4

RING = 4
P_PROJ = RING
FIRST = {("k", 0, 0): 2, ("q", 0, 0): 3, ("v", 0, 0): 0, ("v", 0, 1): 1}
HALF = GN // 2
HIDDEN = 2 * FT
MLP_RING = 3
HID_SLOTS = 4

AT_TURN = 2
AT_RDEN, AT_MIX, AT_SCALE, AT_PROJ, AT_STATS, AT_Z, AT_LNT = 4, 6, 7, 9, 10, 11, 12
CROSS_FROM = 21
AT_MASK = 10
LAST_STEP = CROSS_FROM + QUADS * (GB - 1) + AT_LNT
SIDE = {1: (("k", 0, 1), P_PROJ), 3: (("q", 0, 1), P_PROJ), 15: (("k", 1, 0), P_PROJ),
        17: (("v", 1, 1), 1), 18: (("q", 1, 0), 0), 19: (("k", 1, 1), 2), 20: (("v", 1, 0), 3),
        26: (("q", 1, 1), P_PROJ)}
LOW, HIGH = range(0, 2), range(2, COPIES)
UNITS = list(FIRST) + [unit for unit, _ in SIDE.values()]
IN_BANK = [[u for u, r in list(FIRST.items()) + list(SIDE.values()) if r == bank] for bank in range(RING + 1)]
MOVED = [len(units) + len(range(r, HIDDEN, MLP_RING)) * (r < MLP_RING)
         for r, units in enumerate(IN_BANK)]
ROPED = [u for u in UNITS if u[0] != "v"]
SWAP_LAG = 1
SUM_AT = {7: ("q", 0, 1), 20: ("q", 1, 0), 28: ("q", 1, 1)}
MASK_AT = {6: ("k", 0, 1), 19: ("k", 1, 0), 24: ("k", 1, 1)}
AT_CTX = 6
SIDE_STEPS = sorted(SIDE)


def mlp_order(half):
    u = [("up", f) for f in range(HID_SLOTS)]
    for f in range(FT):
        u.append(("down", f))
        if f + HID_SLOTS < FT:
            u.append(("up", f + HID_SLOTS))
    return [(kind, FT * half + f) for kind, f in u]


FIRST_HALF, _rest = {}, mlp_order(0)
for _step, _n in zip(range(CROSS_FROM + 17, LAST_STEP + 1), (2, 2, 2, 1, 2, 2, 2, 3)):
    FIRST_HALF[_step], _rest = _rest[:_n], _rest[_n:]
assert not _rest


def batch_at(step, lag):
    for s, start in ((SELF, 0), (CROSS, CROSS_FROM)):
        b, r = divmod(step - start - lag, QUADS)
        if r == 0 and 0 <= b < GB:
            yield s, b


def roped_at(step, lag):
    return [SIDE[t][0] for t in (step - lag,) if t in SIDE and SIDE[t][0] in ROPED]


def quad_at(step, lag):
    for s, start in ((SELF, 0), (CROSS, CROSS_FROM)):
        if 0 <= step - start - lag < STEPS:
            yield s, step - start - lag


def build_blocks(nc, a, x_mid, gates_dram, out):
    ctx = ExitStack()
    with ctx:
        def sb(name, shape, dt=F32):
            return ctx.enter_context(nc.sbuf_tensor(name, shape, dt))

        def bank(name):
            return ctx.enter_context(nc.psum_tensor(name, [P, 512], F32))

        def sem(name):
            return ctx.enter_context(nc.semaphore(name))

        w_hi = sb("w_hi", [P, W_ALL], F32R)
        w_lo = sb("w_lo", [P, W_ALL], F32R)
        ident = sb("ident", [P, P])
        head_mask = sb("head_mask", [P, COPIES])
        cos_t = sb("cos_t", [P, N])
        sin_t = sb("sin_t", [P, N])
        ones_row = sb("ones_row", [P, P], BF16)
        minus_half = sb("minus_half", [P, 1])
        bias_rows = sb("bias_rows", [P, 6, D])
        bias_cols = sb("bias_cols", [P, 8 + 2 * FT])
        bias_mod = sb("bias_mod", [P, 20])
        mod = sb("mod", [P, 13, LAYERS * B + GB])
        mod_first = sb("mod_first", [P, 5, GB])
        mod_now = sb("mod_now", [P, 8, GB])
        eps_cols = sb("eps_cols", [P, LAYERS])
        cond = sb("cond", [P, CT, B])
        silu = sb("silu", [P, CT, B])
        silu_tmp = sb("silu_tmp", [P, CT, B])
        gate_now = sb("gate_now", [P, GB, 2, D])
        mask_u8 = sb("mask_u8", [P, GN], U8)
        mask_row = sb("mask_row", [P, GN], BF16)
        x_new = sb("x_new", [P, GB, D])
        x = sb("x", [P, GB, D])
        stats = sb("stats", [P, GB, 6])
        mean_var = sb("mean_var", [P, GB, 2])
        var_eps = sb("var_eps", [P, GB])
        rstd = sb("rstd", [P, GB])
        z = sb("z", [P, GB, D])
        xt = sb("xt", [P, 2, CT, N])
        xt_hi = sb("xt_hi", [P, CT, GN], F32R)
        xt_lo = sb("xt_lo", [P, CT, GN], F32R)
        ctxt = sb("ctxt", [P, CT, GN])
        ctx_hi = sb("ctx_hi", [P, CT, GN], F32R)
        ctx_lo = sb("ctx_lo", [P, CT, GN], F32R)
        q_t = sb("q_t", [P, CT, GN])
        k_t = sb("k_t", [P, CT, COPIES, GN])
        v_pad = [sb(f"v_pad{s}", [P, GB, H, 2 * HD]) for s in range(2)]
        raw = sb("raw", [P, 2, GN])
        rot = sb("rot", [P, 2, GN])
        neg_max = sb("neg_max", [P, 3, 4])
        probs = sb("probs", [P, 3, 4, N])
        row_sum = sb("row_sum", [P, 2, H])
        rden = sb("rden", [P, 2, H])
        rden_wide = sb("rden_wide", [P, D])
        rden_t = sb("rden_t", [P, D])
        probs_t = sb("probs_t", [P, 2, QUADS, 4, N])
        heads = sb("heads", [P, 2, CT, N])
        heads_hi = sb("heads_hi", [P, 2, CT, N], F32R)
        heads_lo = sb("heads_lo", [P, 2, CT, N], F32R)
        delta = sb("delta", [P, 2, D])
        gate_bias = raw[0:B, 0, :].rearrange("b (g c) -> b g c", g=2)
        gate_rows = raw[0:B, 1, :].rearrange("b (g c) -> b g c", g=2)
        hid = raw[:, :, 0:HALF]
        hid_hi = sb("hid_hi", [P, HID_SLOTS, HALF], F32R)
        hid_lo = sb("hid_lo", [P, HID_SLOTS, HALF], F32R)
        stage = probs_t[:, :, :, :, :].rearrange("p a q s n -> p (a q s n)")

        ring = [bank(f"ring{r}") for r in range(RING)]
        score_banks = [ring[0], ring[1], bank("third")]
        mix = bank("mix")
        p_proj = bank("p_proj")
        p_ln = bank("p_ln")
        y_mlp = [score_banks[2], ring[3], mix, p_proj]

        c_loaded = sem("c_loaded")
        ready = sem("ready")
        dve_held = sem("dve_held")
        half_made = sem("half_made")
        silu_step = sem("silu_step")
        mod_full = sem("mod_full")
        mod_step = sem("mod_step")
        w_loaded = [sem(f"w_loaded{h}") for h in range(2)]
        w_hi_made = sem("w_hi_made")
        w_lo_made = sem("w_lo_made")
        stored = sem("stored")
        x_loaded = sem("x_loaded")
        ctx_loaded = sem("ctx_loaded")
        side_loaded = sem("side_loaded")
        mask_made = sem("mask_made")
        first_copied = sem("first_copied")
        mod_copied = sem("mod_copied")
        ctx_hi_made = sem("ctx_hi_made")
        ctx_lo_made = sem("ctx_lo_made")
        stats_made = sem("stats_made")
        moments_made = sem("moments_made")
        eps_added = sem("eps_added")
        rstd_made = sem("rstd_made")
        z_made = sem("z_made")
        z_turned = sem("z_turned")
        ln_moved = sem("ln_moved")
        xt_hi_made = sem("xt_hi_made")
        xt_lo_made = sem("xt_lo_made")
        first_full = sem("first_full")
        up_full = sem("up_full")
        moved = [sem(f"moved{r}") for r in range(RING)] + [sem("moved_p_proj")]
        side_full = sem("side_full")
        swapped = sem("swapped")
        cos_made = sem("cos_made")
        sin_made = sem("sin_made")
        sin_keys = sem("sin_keys")
        keys_summed = sem("keys_summed")
        keys_low = sem("keys_low")
        keys_high = sem("keys_high")
        queries_made = sem("queries_made")
        scored = sem("scored")
        max_made = sem("max_made")
        exps_made = sem("exps_made")
        probs_turned = sem("probs_turned")
        probs_moved = sem("probs_moved")
        rden_made = sem("rden_made")
        rden_spread = sem("rden_spread")
        mixed = sem("mixed")
        rden_turned = sem("rden_turned")
        rden_moved = sem("rden_moved")
        heads_scaled = sem("heads_scaled")
        heads_hi_made = sem("heads_hi_made")
        heads_lo_made = sem("heads_lo_made")
        projected = sem("projected")
        hid_used = sem("hid_used")
        fc2_full = sem("fc2_full")
        y_moved = sem("y_moved")
        gated = sem("gated")
        x_updated = sem("x_updated")
        hid_hi_made = sem("hid_hi_made")
        hid_lo_made = sem("hid_lo_made")

        GATE_STORES = 1
        CONST_LOADS = 13

        def moved_by(eng, it, unit):
            bank, = (r for r, units in enumerate(IN_BANK) if unit in units)
            eng.wait_ge(moved[bank], it * MOVED[bank] + IN_BANK[bank].index(unit) + 1)

        def up_moved(eng, it, u):
            r = u % MLP_RING
            eng.wait_ge(moved[r], it * MOVED[r] + len(IN_BANK[r]) + u // MLP_RING + 1)

        def y_out(eng, it, j):
            eng.wait_ge(y_moved, it * 12 + 1 + j + 1)

        def x_ready(eng, layer, g, j):
            if layer == 0:
                eng.wait_ge(x_updated, g * 12 + j + 1)
            elif j < 8:
                y_out(eng, g + NG, j)
            else:
                eng.wait_ge(x_updated, g * 4 + 12 * NG + j - 8 + 1)

        block = ctx.enter_context(nc.Block())

        @block.sync
        def _(sp):
            for dst, src in (
                (cond[:], a["condT"].rearrange("(t p) b -> p t b", p=P)),
                (stage[:, 0:CT * 6 * D].rearrange("p (t n) -> p t n", t=CT),
                 a["L0_xcond_ada_w"].rearrange("(t p) n -> p t n", p=P)),
                (k_t[:].rearrange("p t e n -> p (t e n)")[:, 0:2 * CT * 2 * D].rearrange("p (m t n) -> p m t n", m=2, t=CT),
                 a["ln_wT"][0:2].rearrange("m (t p) n -> p m t n", p=P)),
                (q_t[:], a["ln_wT"][2].rearrange("(t p) n -> p t n", p=P)),
                (bias_mod[:], a["bias_mod"]),
                (gate_bias, a["gate_bias"].partition_broadcast(B)),
                (ident[:], a["ident"]),
                (head_mask[:], a["head_mask"]),
                (cos_t[:], a["cos_t"]),
                (sin_t[:], a["sin_t"]),
                (bias_rows[:], a["bias_rows"].partition_broadcast(P)),
                (bias_cols[:], a["bias_cols"]),
            ):
                sp.dma_start(dst, src).then_inc(c_loaded, 16)
            sp.dma_start(ctxt[:], a["ctxT"][:, 0:GN].rearrange("(t p) n -> p t n", p=P)).then_inc(ctx_loaded, 16)
            sp.dma_start(x_new[:], a["x"][0:GN, :].rearrange("(b p) c -> p b c", p=P)).then_inc(x_loaded, 16)

            def load_weights(layer):
                for c, parts in enumerate(WEIGHTS[layer]):
                    n = 4 * layer + c
                    if n >= 2 and c >= 2:
                        sp.wait_ge(w_hi_made, n - 1)
                        sp.wait_ge(w_lo_made, n - 1)
                    for name, col, kt, width in parts:
                        at = col - c * CHUNK + (c % 2) * CHUNK
                        dst = stage[:, at:at + kt * width].rearrange("p (t n) -> p t n", t=kt)
                        sp.dma_start(dst, a[name].rearrange("(t p) n -> p t n", p=P)).then_inc(w_loaded[c % 2], 16)

            sp.wait_ge(mod_full, 2)
            load_weights(0)
            sp.wait_ge(y_moved, 1)
            sp.dma_start(gates_dram, gate_rows).then_inc(stored, 16)
            sp.wait_ge(stored, 16)

            def side(i):
                sp.dma_start(gate_now[:].rearrange("p b g c -> p (b g c)"),
                             gates_dram[bass.ds(i * GB, GB)].rearrange("b g c -> (b g c)")
                             .partition_broadcast(P)).then_inc(side_loaded, 16)
                sp.dma_start(mask_u8[:].bitcast(U32), a["mask"][bass.ds(i * (GN // 4), GN // 4)].partition_broadcast(P)).then_inc(side_loaded, 16)

            def load_ctx(i):
                sp.dma_start(ctxt[:], a["ctxT"][:, bass.ds(i * GN, GN)].rearrange("(t p) n -> p t n", p=P))\
                  .then_inc(ctx_loaded, 16)

            def load_x(src, i):
                sp.dma_start(x_new[:], src[bass.ds(i * GN, GN), :].rearrange("(b p) c -> p b c", p=P))\
                  .then_inc(x_loaded, 16)

            def store_x(dst, layer, i):
                x_ready(sp, layer, i, 11)
                sp.dma_start(dst[bass.ds(i * GN, GN), :].rearrange("(b p) c -> p b c", p=P), x[:]).then_inc(stored, 16)

            side(0)
            with sp.Fori(0, NG - 1) as i:
                sp.wait_ge(ctx_lo_made, i + 1)
                load_ctx(i + 1)
                x_ready(sp, 0, i, 3)
                load_x(a["x"], i + 1)
                x_ready(sp, 0, i, 11)
                side(i + 1)
                store_x(x_mid, 0, i)
            sp.wait_ge(ctx_lo_made, NG)
            load_ctx(0)
            x_ready(sp, 0, NG - 1, 3)
            sp.wait_ge(stored, 16 * (GATE_STORES + NG - 1))
            load_x(x_mid, 0)
            sp.wait_ge(mixed, NG * 8)
            load_weights(1)
            x_ready(sp, 0, NG - 1, 11)
            store_x(x_mid, 0, NG - 1)
            sp.wait_ge(stored, 16 * (GATE_STORES + NG))
            with sp.Fori(0, NG - 1) as i:
                sp.wait_ge(ctx_lo_made, i + NG + 1)
                load_ctx(i + 1)
                x_ready(sp, 1, i, 3)
                load_x(x_mid, i + 1)
                store_x(out, 1, i)
            x_ready(sp, 1, NG - 1, 3)
            load_x(x_mid, 0)
            store_x(out, 1, NG - 1)
            sp.wait_ge(stored, 16 * (GATE_STORES + LAYERS * NG))
            sp.wait_ge(x_loaded, 16 * (LAYERS * NG + 1))

        @block.tensor
        def _(pe):
            def product(dst, lhs, rhs, first, last):
                pe.matmul(dst, lhs[1], rhs[0], start=first, stop=False)
                pe.matmul(dst, lhs[0], rhs[1], start=False, stop=False)
                return pe.matmul(dst, lhs[0], rhs[0], start=False, stop=last)

            def w(col, kt, stride, lo, width):
                c = col + kt * stride + lo
                return w_hi[:, c:c + width], w_lo[:, c:c + width]

            def turn_z(it, k, b):
                pe.wait_ge(z_made, it * 12 + 4 * k + b + 1)
                if k > 0:
                    p_ln_free(it, z=True, n=4 * k + b)
                elif not (isinstance(it, int) and b == 0):
                    pe.wait_ge(ln_moved, it * 12 + b)
                for c in range(CT):
                    mm = pe.transpose(p_ln[:, c * P:(c + 1) * P], z[:, b, c * P:(c + 1) * P], ident[:])
                mm.then_inc(z_turned, 1)

            def make_unit(it, unit, dst):
                kind, s, half = unit
                if s == CROSS and kind != "q":
                    pe.wait_ge(ctx_hi_made, it + 1)
                    pe.wait_ge(ctx_lo_made, it + 1)
                    hi, lo = ctx_hi, ctx_lo
                else:
                    pe.wait_ge(xt_hi_made, it * 12 + 4 * s + 2 * half + 2)
                    pe.wait_ge(xt_lo_made, it * 12 + 4 * s + 2 * half + 2)
                    hi, lo = xt_hi, xt_lo
                col, stride, at = {("k", SELF): (W_QKV, 3 * D, D), ("q", SELF): (W_QKV, 3 * D, 0),
                                   ("v", SELF): (W_QKV, 3 * D, 2 * D), ("k", CROSS): (W_KV, 2 * D, 0),
                                   ("v", CROSS): (W_KV, 2 * D, D), ("q", CROSS): (W_Q, D, 0)}[kind, s]
                for part in range(2):
                    for c in range(CT):
                        if kind == "v":
                            cols = slice((2 * half + part) * N, (2 * half + part + 1) * N)
                            lhs, rhs = (hi[:, c, cols], lo[:, c, cols]), w(col, c, stride, at, D)
                        else:
                            cols = slice(half * HALF, (half + 1) * HALF)
                            lhs, rhs = w(col, c, stride, at + part * P, P), (hi[:, c, cols], lo[:, c, cols])
                        mm = product(dst[:, part * HALF:(part + 1) * HALF], lhs, rhs, c == 0, c == CT - 1)
                return mm

            def side_unit(it, step):
                unit, r = SIDE[step]
                if step == SIDE_STEPS[0]:
                    y_out(pe, it - 1, 11)
                elif r == P_PROJ:
                    p_proj_free(it, step)
                elif r < 2:
                    pe.wait_ge(exps_made, it * 32 + max(g for g in range(STEPS) if g % 3 == r) + 1)
                else:
                    pe.wait_ge(probs_moved, it * 32 + STEPS - 3 + r)
                make_unit(it, unit, p_proj if r == P_PROJ else ring[r]).then_inc(side_full, 1)

            def p_ln_free(it, z, n):
                uses = sorted([((CROSS_FROM if j >= 4 else 0) + QUADS * (j % 4) + AT_MIX, 0, j) for j in range(8)]
                              + [((CROSS_FROM if j >= 8 else 0) + QUADS * (j % 4) + AT_LNT, 1, j) for j in range(4, 12)])
                at = [u[1:] for u in uses].index((int(z), n))
                if at == 0:
                    pe.wait_ge(ln_moved, it * 12 + 4)
                elif uses[at - 1][1]:
                    pe.wait_ge(ln_moved, it * 12 + uses[at - 1][2] + 1)
                else:
                    pe.wait_ge(rden_moved, it * 8 + uses[at - 1][2] + 1)

            def p_proj_free(it, step, projection=False):
                sides = [t for t in SIDE_STEPS if SIDE[t][1] == P_PROJ]
                uses = sorted([(t, 1, n) for n, t in enumerate(sides)]
                              + [((CROSS_FROM if j >= 4 else 0) + QUADS * (j % 4) + AT_PROJ, 0, j) for j in range(8)])
                at = [n for n, (t, side, _) in enumerate(uses) if t == step and side == (not projection)][0]
                _, side, n = uses[at - 1]
                if side:
                    moved_by(pe, it, SIDE[sides[n]][0])
                else:
                    y_out(pe, it, n)

            def scores(it, layer, s, g):
                b, q = divmod(g, QUADS)
                if g % (STEPS // 2) == 0:
                    half = g // (STEPS // 2)
                    pe.wait_ge(keys_low, it * 4 + 2 * s + half + 1)
                    if layer == 0:
                        moved_by(pe, it, ("q", s, half))
                    else:
                        pe.wait_ge(queries_made, (it - NG) * 4 + 2 * s + half + 1)
                if g % (STEPS // 2) == 1:
                    pe.wait_ge(keys_high, it * 4 + 2 * s + g // (STEPS // 2) + 1)
                G = s * STEPS + g
                if g < 3 and G % 3 < 2:
                    moved_by(pe, it, IN_BANK[G % 3][-s])
                if G >= 3:
                    pe.wait_ge(exps_made, it * 32 + G - 2)
                dst = score_banks[G % 3]
                r = slice(64 * (q // 2), 64 * (q // 2) + 64)
                copies = slice(2 * (q % 2), 2 * (q % 2) + 2)
                masked = layer == 0 and s == CROSS
                if masked:
                    if g == 0:
                        pe.wait_ge(mask_made, it + 1)
                    rows = mask_row[:, b * N:(b + 1) * N].unsqueeze(1).broadcast_to([P, 4, N])
                    pe.matmul(dst[:].rearrange("p (h n) -> p h n", h=4), ones_row[:], rows,
                              start=True, stop=False, skip_group_check=True)
                for t in range(CT):
                    mm = pe.matmul(dst[:, t * 2 * N:(t + 1) * 2 * N].rearrange("p (e n) -> p e n", e=2),
                                   q_t[r, t, b * N:(b + 1) * N], k_t[r, t, copies, b * N:(b + 1) * N],
                                   start=not masked, stop=True, skip_group_check=masked)
                mm.then_inc(scored, 1)

            def turn_probs(it, s, g):
                pe.wait_ge(exps_made, it * 32 + s * STEPS + g + 1)
                if g < 2:
                    moved_by(pe, it, IN_BANK[2 + g][-s])
                if g >= 2 or s == CROSS:
                    pe.wait_ge(probs_moved, it * 32 + s * STEPS + g - 1)
                for h in range(4):
                    mm = pe.transpose(ring[2 + g % 2][:, h * N:(h + 1) * N], probs[:, (s * STEPS + g) % 3, h, :], ident[:])
                mm.then_inc(probs_turned, 1)

            def mix_values(it, s, b):
                pe.wait_ge(probs_moved, it * 32 + s * STEPS + QUADS * b + QUADS)
                moved_by(pe, it, ("v", s, b // 2))
                if 4 * s + b >= 1:
                    pe.wait_ge(heads_scaled, it * 8 + 4 * s + b)
                dst = mix
                for t in range(CT):
                    for e in range(2):
                        for q in range(QUADS):
                            mm = pe.matmul(dst[32 * q:32 * q + 32, t * N:(t + 1) * N],
                                           v_pad[s][:, b, 8 * t + 2 * q + e, :],
                                           probs_t[:, b % 2, q, 2 * t + e, :],
                                           start=(e == 0), stop=(e == 1), tile_position=(0, 32 * q))
                mm.then_inc(mixed, 1)

            def turn_rden(it, s, b):
                pe.wait_ge(rden_spread, it * 8 + 4 * s + b + 1)
                p_ln_free(it, z=False, n=4 * s + b)
                for t in range(CT):
                    mm = pe.transpose(p_ln[:, t * P:(t + 1) * P], rden_wide[:, t * P:(t + 1) * P], ident[:])
                mm.then_inc(rden_turned, 1)

            def project(it, s, b):
                j = 4 * s + b
                pe.wait_ge(heads_hi_made, it * 8 + j + 1)
                pe.wait_ge(heads_lo_made, it * 8 + j + 1)
                p_proj_free(it, (CROSS_FROM if s else 0) + QUADS * b + AT_PROJ, projection=True)
                for t in range(CT):
                    mm = product(p_proj[:, 0:D], (heads_hi[:, b % 2, t, :], heads_lo[:, b % 2, t, :]),
                                 w(W_SA if s == SELF else W_CA, t, D, 0, D), t == 0, t == CT - 1)
                mm.then_inc(projected, 1)

            def up(it, u):
                if u == 2:
                    pe.wait_ge(probs_moved, it * 32 + 32)
                if u >= MLP_RING:
                    up_moved(pe, it, u - MLP_RING)
                half, f = divmod(u, FT)
                if f == 0:
                    pe.wait_ge(xt_hi_made, it * 12 + 8 + 2 * half + 2)
                    pe.wait_ge(xt_lo_made, it * 12 + 8 + 2 * half + 2)
                cols = slice(half * HALF, (half + 1) * HALF)
                for c in range(CT):
                    mm = product(ring[u % MLP_RING][:, 0:HALF], w(W_F1, c, DF, f * P, P),
                                 (xt_hi[:, c, cols], xt_lo[:, c, cols]), c == 0, c == CT - 1)
                mm.then_inc(up_full, 1)

            def down(it, u):
                half, f = divmod(u, FT)
                pe.wait_ge(hid_hi_made, it * HIDDEN + u + 1)
                pe.wait_ge(hid_lo_made, it * HIDDEN + u + 1)
                if f == 0 and half == 0:
                    pe.wait_ge(probs_moved, it * 32 + 32)
                elif f == 0:
                    pe.wait_ge(heads_scaled, it * 8 + 8)
                    y_out(pe, it, 7)
                slot = u % HID_SLOTS
                for k in range(2):
                    mm = product(y_mlp[2 * half + k][:, 0:D],
                                 (hid_hi[:, slot, k * N:(k + 1) * N], hid_lo[:, slot, k * N:(k + 1) * N]),
                                 w(W_F2, f, D, 0, D), f == 0, f == FT - 1)
                    if f == FT - 1 and k == 0:
                        mm.then_inc(fc2_full, 1)
                if f == FT - 1:
                    mm.then_inc(fc2_full, 1)
                else:
                    mm.then_inc(hid_used, 1)

            def mlp(it, kind, u):
                (up if kind == "up" else down)(it, u)

            def attention(it, layer):
                for step in range(LAST_STEP + 1):
                    for s, g in quad_at(step, 0):
                        scores(it, layer, s, g)
                    for s, g in quad_at(step, AT_TURN):
                        turn_probs(it, s, g)
                    for s, b in batch_at(step, AT_MIX):
                        turn_rden(it, s, b)
                        mix_values(it, s, b)
                    for s, b in batch_at(step, AT_PROJ):
                        project(it, s, b)
                    for s, b in batch_at(step, AT_LNT):
                        turn_z(it, s + 1, b)
                    if step in SIDE:
                        side_unit(it, step)
                    for unit in FIRST_HALF.get(step, ()):
                        mlp(it, *unit)

            pe.wait_ge(c_loaded, 16 * (CONST_LOADS - 1))
            pe.wait_ge(silu_step, 4)
            ada = stage[:, 0:CT * 6 * D].rearrange("p (t n) -> p t n", t=CT)
            lnw = [k_t[:].rearrange("p t e n -> p (t e n)")[:, 0:2 * CT * 2 * D].rearrange("p (m t n) -> p m t n", m=2, t=CT)[:, m]
                   for m in range(2)] + [q_t[:]]
            n = 0
            for chunk in (1, 0, 4, 3):
                for o in range(CT):
                    for c in range(CT):
                        mm = pe.matmul(mix[:, n * B:(n + 1) * B],
                                       ada[:, c, chunk * D + o * P:chunk * D + (o + 1) * P], silu[:, c, :],
                                       start=(c == 0), stop=(c == CT - 1))
                    n += 1
            for g, chunk in enumerate((2, 5)):
                for c in range(CT):
                    mm = pe.matmul(p_proj[0:B, g * D:(g + 1) * D], silu[:, c, :],
                                   ada[:, c, chunk * D:(chunk + 1) * D], start=(c == 0), stop=(c == CT - 1))
            mm.then_inc(mod_full, 1)
            n = 0
            for k in range(3):
                for half in range(2):
                    for o in range(CT):
                        for c in range(CT):
                            mm = pe.matmul(score_banks[2][:, n * B:(n + 1) * B],
                                           lnw[k][:, c, half * D + o * P:half * D + (o + 1) * P], cond[:, c, :],
                                           start=(c == 0), stop=(c == CT - 1))
                        n += 1
            mm.then_inc(mod_full, 1)

            for b in range(GB):
                turn_z(0, 0, b)
            for layer in range(LAYERS):
                pe.wait_ge(w_hi_made, 4 * layer + 4)
                pe.wait_ge(w_lo_made, 4 * layer + 4)
                with pe.Fori(0, NG) as i:
                    it = i + layer * NG
                    for unit, r in FIRST.items():
                        make_unit(it, unit, ring[r]).then_inc(first_full, 1)
                    attention(it, layer)
                    for kind, u in mlp_order(1):
                        mlp(it, kind, u)
                        for b in {("up", 11): (0,), ("down", 8): (1,), ("up", 15): (2,), ("down", 13): (3,)}.get((kind, u), ()):
                            turn_z(it + 1, 0, b)

        @block.scalar
        def _(act):
            def modulate(it, k, b):
                act.wait_ge(z_turned, it * 12 + 4 * k + b + 1)
                if not (isinstance(it, int) and b < 2):
                    act.wait_ge(xt_lo_made, it * 12 + 4 * k + b - 1)
                if k == 0 and b == 0:
                    act.wait_ge(first_copied, it + 1)
                if k == 1 and b == 0:
                    act.wait_ge(mod_copied, it + 1)
                for c in range(CT):
                    table, m = (mod_first, 0) if k == 0 else (mod_now, 4 * (k - 1))
                    op = act.activation(xt[:, b % 2, c, :], p_ln[:, c * P:(c + 1) * P], ACT.Identity,
                                        scale=table[:, m + c, b:b + 1], bias=table[:, m + 2 + c, b:b + 1])
                op.then_inc(ln_moved, 1)
                act.wait_ge(ln_moved, it * 12 + 4 * k + b + 1)
                act.copy(xt_hi[:, :, b * N:(b + 1) * N], xt[:, b % 2, :, :]).then_inc(xt_hi_made, 1)

            def move_unit(it, layer, unit, src, signal):
                kind, s, half = unit
                m = 2 * s + half
                if layer == 0 and kind == "q":
                    for t in range(CT):
                        op = act.activation(q_t[:, t, half * HALF:(half + 1) * HALF], src[:, t * HALF:(t + 1) * HALF],
                                            ACT.Identity, scale=SCALE,
                                            bias=bias_cols[:, 4 + 2 * s + t:5 + 2 * s + t])
                    op.then_inc(signal, 1)
                elif layer == 0:
                    if m:
                        act.wait_ge(keys_high, it * 4 + m)
                    for t in range(CT):
                        op = act.activation(raw[:, 0, t * HALF:(t + 1) * HALF], src[:, t * HALF:(t + 1) * HALF],
                                            ACT.Identity, bias=bias_cols[:, 2 * s + t:2 * s + t + 1])
                    op.then_inc(signal, 1)
                elif kind == "v":
                    for k in range(2):
                        for e in range(2):
                            dst = v_pad[s][:, 2 * half + k].rearrange("p h w -> p (h w)")\
                                .rearrange("p (a e w) -> p a e w", a=H // 2, e=2)[:, :, e, e * HD:(e + 1) * HD]
                            op = act.copy(dst, src[:, k * D:(k + 1) * D].rearrange("p (a e d) -> p a e d", a=H // 2, e=2)
                                          [:, :, e, :])
                    op.then_inc(signal, 1)
                else:
                    if m:
                        act.wait_ge(queries_made if kind == "q" else keys_summed, (it - NG) * 4 + m)
                    act.activation(raw[:, int(kind == "q"), :], src[:], ACT.Copy, scale=SCALE if kind == "q" else 1.0)\
                       .then_inc(signal, 1)

            def move_first(it, layer, n):
                unit, r = list(FIRST.items())[n]
                if unit[0] != "v" or layer == 1:
                    act.wait_ge(first_full, it * len(FIRST) + n + 1)
                    move_unit(it, layer, unit, ring[r], moved[r])
                if n == (0 if layer == 0 else 2):
                    low_keys(it, layer, list(FIRST)[0])

            def low_keys(it, layer, unit):
                _, s, half = unit
                if layer == 0:
                    moved_by(act, it, unit)
                    src = raw
                else:
                    act.wait_ge(keys_summed, (it - NG) * 4 + 2 * s + half + 1)
                    src = rot
                for e in LOW:
                    op = act.activation(k_t[:, :, e, half * HALF:(half + 1) * HALF],
                                        src[:, 0, :].rearrange("p (t n) -> p t n", t=CT),
                                        ACT.Copy, scale=head_mask[:, e:e + 1])
                op.then_inc(keys_low, 1)

            def move_side(it, layer, step):
                unit, r = SIDE[step]
                if unit[0] != "v":
                    act.wait_ge(side_full, it * len(SIDE) + SIDE_STEPS.index(step) + 1)
                    move_unit(it, layer, unit, (ring + [p_proj])[r], moved[r])
                    if layer == 0 and unit[0] == "k":
                        low_keys(it, layer, unit)

            def gelu(it, layer, u):
                act.wait_ge(up_full, it * HIDDEN + u + 1)
                if u >= 2:
                    act.wait_ge(hid_lo_made, it * HIDDEN + u - 1)
                m = 8 + FT * layer + u % FT
                act.activation(hid[:, u % 2, :], ring[u % MLP_RING][:, 0:HALF], ACT.Gelu, bias=bias_cols[:, m:m + 1])\
                   .then_inc(moved[u % MLP_RING], 1)

            def exps(it, s, g):
                b, q = divmod(g, QUADS)
                G = s * STEPS + g
                act.wait_ge(max_made, it * 32 + G + 1)
                if G >= 3:
                    act.wait_ge(probs_turned, it * 32 + G - 2)
                for h in range(4):
                    head = 8 * (h // 2) + 2 * q + h % 2
                    op = act.activation(probs[:, G % 3, h, :], score_banks[G % 3][:, h * N:(h + 1) * N], ACT.Exp,
                                        bias=neg_max[:, G % 3, h:h + 1], accum_out=row_sum[:, b % 2, head:head + 1])
                op.then_inc(exps_made, 1)

            def move_rden(it, s, b):
                act.wait_ge(rden_turned, it * 8 + 4 * s + b + 1)
                act.copy(rden_t[:], p_ln[:, 0:D]).then_inc(rden_moved, 1)

            def attention(it, layer):
                for step in range(LAST_STEP + 1):
                    for s, g in quad_at(step, 0):
                        exps(it, s, g)
                    for s, b in batch_at(step, AT_MIX):
                        move_rden(it, s, b)
                    for s, b in batch_at(step, AT_LNT):
                        modulate(it, s + 1, b)
                    if step in SIDE:
                        move_side(it, layer, step)
                    if layer == 1 and step in MASK_AT:
                        low_keys(it, layer, MASK_AT[step])
                    if step == AT_CTX:
                        act.wait_ge(ctx_loaded, (it + 1) * 16)
                        act.copy(ctx_hi[:], ctxt[:]).then_inc(ctx_hi_made, 1)
                    for kind, u in FIRST_HALF.get(step, ()):
                        if kind == "up":
                            gelu(it, layer, u)

            act.wait_ge(c_loaded, 16 * (CONST_LOADS - 1))
            act.activation(silu_tmp[:], cond[:], ACT.Exp, scale=-1.0).then_inc(silu_step, 1)
            def split_weights(layer):
                for c in range(4):
                    n = 4 * layer + c
                    act.wait_ge(w_loaded[c % 2], 16 * W_LOADS[n])
                    act.copy(w_hi[:, c * CHUNK:(c + 1) * CHUNK], stage[:, (c % 2) * CHUNK:(c % 2 + 1) * CHUNK])\
                       .then_inc(w_hi_made, 1)

            split_weights(0)
            for b in range(GB):
                modulate(0, 0, b)
            for layer in range(LAYERS):
                if layer:
                    split_weights(1)
                with act.Fori(0, NG) as i:
                    it = i + layer * NG
                    for n in range(len(FIRST)):
                        move_first(it, layer, n)
                    attention(it, layer)
                    for kind, u in mlp_order(1):
                        if kind == "up":
                            gelu(it, layer, u)
                            for b in {10: (0,), 11: (1,), 15: (2, 3)}.get(u, ()):
                                modulate(it + 1, 0, b)

        @block.vector
        def _(dve):
            def moments(it, layer, k, b):
                j = 4 * k + b
                if k == 0:
                    dve.wait_ge(x_loaded, (it + 1) * 16)
                else:
                    x_ready(dve, layer, it - layer * NG, j - 4)
                src = x_new if k == 0 else x
                dve.bn_stats(stats[:, b, :], src[:, b, :]).then_inc(stats_made, 1)
                dve.wait_ge(stats_made, it * 12 + j + 1)
                dve.sem_inc(dve_held, 1)
                dve.bn_aggr(mean_var[:, b, :], stats[:, b, :]).then_inc(moments_made, 1)

            def normalise(it, k, b):
                dve.wait_ge(rstd_made, it * 12 + 4 * k + b + 1)
                src = x_new if k == 0 else x
                dve.tensor_scalar(z[:, b, :], src[:, b, :], mean_var[:, b, 0:1], rstd[:, b:b + 1],
                                  ALU.subtract, ALU.mult).then_inc(z_made, 1)

            def put_values(layer, s, b, src):
                for e in range(2):
                    dst = v_pad[s][:, b].rearrange("p h w -> p (h w)").rearrange("p (a e w) -> p a e w", a=H // 2, e=2)\
                        [:, :, e, e * HD:(e + 1) * HD]
                    heads_of = src.rearrange("p (a e d) -> p a e d", a=H // 2, e=2)[:, :, e, :]
                    if layer == 0:
                        bias = bias_rows[:, s, :].rearrange("p (a e d) -> p a e d", a=H // 2, e=2)[:, :, e, :]
                        op = dve.tensor_tensor(dst, heads_of, bias, ALU.add)
                    else:
                        op = dve.tensor_copy(dst, heads_of)
                return op

            def swap(it, unit):
                kind, s, half = unit
                which = int(kind == "q")
                if kind == "k" and unit not in FIRST:
                    dve.wait_ge(keys_high, it * 4 + 2 * s + half)
                    dve.wait_ge(keys_low, it * 4 + 2 * s + half)
                moved_by(dve, it, unit)
                dve.sem_inc(dve_held, 1)
                dve.stream_shuffle(rot[:, which, :], raw[:, which, :], SWAP).then_inc(swapped, 1)

            def times_sin(it, unit):
                which = int(unit[0] == "q")
                dve.wait_ge(swapped, (it - NG) * len(ROPED) + ROPED.index(unit) + 1)
                table = sin_t[:].unsqueeze(1).broadcast_to([P, GB, N])
                rot3 = rot[:, which, :].rearrange("p (b n) -> p b n", b=GB)
                dve.tensor_tensor(rot3, rot3, table, ALU.mult).then_inc(sin_made, 1)

            def sum_rotated(it, unit):
                kind, s, half = unit
                g = it - NG
                dve.wait_ge(sin_made, g * 5 + (1 if kind == "k" else 2 + 2 * s + half))
                dve.wait_ge(cos_made, g * len(ROPED) + ROPED.index(unit) + 1)
                if kind == "k":
                    dve.tensor_tensor(rot[:, 0, :], raw[:, 0, :], rot[:, 0, :], ALU.add).then_inc(keys_summed, 1)
                else:
                    dve.tensor_tensor(q_t[:, :, half * HALF:(half + 1) * HALF],
                                      raw[:, 1, :].rearrange("p (t n) -> p t n", t=CT),
                                      rot[:, 1, :].rearrange("p (t n) -> p t n", t=CT), ALU.add).then_inc(queries_made, 1)

            def high_keys(it, layer, unit):
                _, s, half = unit
                if layer == 0:
                    moved_by(dve, it, unit)
                    src = raw
                else:
                    dve.wait_ge(keys_summed, (it - NG) * 4 + 2 * s + half + 1)
                    src = rot
                for e in HIGH:
                    op = dve.tensor_scalar(k_t[:, :, e, half * HALF:(half + 1) * HALF],
                                           src[:, 0, :].rearrange("p (t n) -> p t n", t=CT),
                                           head_mask[:, e:e + 1], None, ALU.mult)
                op.then_inc(keys_high, 1)

            def move_values(it, layer, unit, src, signal):
                _, s, half = unit
                for k in range(2):
                    op = put_values(layer, s, 2 * half + k, src[:, k * D:(k + 1) * D])
                op.then_inc(signal, 1)

            def move_first(it, n):
                unit, r = list(FIRST.items())[n]
                if unit[0] == "k":
                    high_keys(it, 0, unit)
                elif unit[0] == "v":
                    dve.wait_ge(first_full, it * len(FIRST) + n + 1)
                    move_values(it, 0, unit, ring[r], moved[r])

            def move_side(it, layer, step):
                unit, r = SIDE[step]
                if unit[0] == "v":
                    dve.wait_ge(side_full, it * len(SIDE) + SIDE_STEPS.index(step) + 1)
                    move_values(it, layer, unit, (ring + [p_proj])[r], moved[r])
                elif unit[0] == "k" and layer == 0:
                    high_keys(it, 0, unit)

            def row_max(it, s, g):
                dve.wait_ge(scored, it * 32 + s * STEPS + g + 1)
                G = s * STEPS + g
                dve.tensor_reduce(neg_max[:, G % 3, :], score_banks[G % 3][:].rearrange("p (h n) -> p h n", h=4),
                                  AX.X, ALU.max, negate=True).then_inc(max_made, 1)

            def move_probs(it, s, g):
                b, q = divmod(g, QUADS)
                dve.wait_ge(probs_turned, it * 32 + s * STEPS + g + 1)
                dve.tensor_copy(probs_t[:, b % 2, q].rearrange("p h n -> p (h n)"), ring[2 + g % 2][:])\
                   .then_inc(probs_moved, 1)

            def make_rden(it, s, b):
                j = 4 * s + b
                dve.wait_ge(exps_made, it * 32 + s * STEPS + QUADS * b + QUADS)
                dve.reciprocal(rden[:, b % 2, :], row_sum[:, b % 2, :]).then_inc(rden_made, 1)
                dve.wait_ge(rden_made, it * 8 + j + 1)
                dve.tensor_copy(rden_wide[:].rearrange("p (h d) -> p h d", h=H),
                                rden[:, b % 2, :].unsqueeze(2).broadcast_to([P, H, HD])).then_inc(rden_spread, 1)

            def scale_heads(it, s, b):
                j = 4 * s + b
                dve.wait_ge(mixed, it * 8 + j + 1)
                dve.wait_ge(rden_moved, it * 8 + j + 1)
                dve.tensor_tensor(heads[:, b % 2].rearrange("p t n -> p (t n)"), mix[:, 0:D], rden_t[:],
                                  ALU.mult).then_inc(heads_scaled, 1)
                dve.wait_ge(heads_scaled, it * 8 + j + 1)
                dve.tensor_copy(heads_hi[:, b % 2], heads[:, b % 2]).then_inc(heads_hi_made, 1)
                dve.wait_ge(heads_hi_made, it * 8 + j + 1)
                dve.tensor_tensor(heads_lo[:, b % 2], heads[:, b % 2], heads_hi[:, b % 2].bitcast(F32), ALU.subtract)\
                   .then_inc(heads_lo_made, 1)

            def take_output(it, layer, j):
                b = j % 4
                if j < 8:
                    dve.wait_ge(projected, it * 8 + j + 1)
                    src = p_proj[:, 0:D]
                else:
                    dve.wait_ge(fc2_full, it * 4 + b + 1)
                    src = y_mlp[b][:, 0:D]
                if j == 0:
                    dve.wait_ge(stored, it * 16 + 16 * GATE_STORES)
                if layer == 1 and j < 8:
                    dve.tensor_tensor(x[:, b, :], src, x_new[:, b, :] if j < 4 else x[:, b, :], ALU.add)\
                       .then_inc(y_moved, 1)
                else:
                    if j >= 2:
                        if layer == 0:
                            dve.wait_ge(x_updated, it * 12 + j - 1)
                        elif j >= 10:
                            dve.wait_ge(x_updated, (it - NG) * 4 + 12 * NG + j - 9)
                    row = 2 + j // 4 if layer == 0 else 5
                    dve.tensor_tensor(delta[:, j % 2, :], src, bias_rows[:, row, :], ALU.add).then_inc(y_moved, 1)

            def split_hidden(it, u):
                up_moved(dve, it, u)
                if u >= HID_SLOTS:
                    dve.wait_ge(*slot_free(it, u - HID_SLOTS))
                dve.tensor_copy(hid_hi[:, u % HID_SLOTS, :], hid[:, u % 2, :]).then_inc(hid_hi_made, 1)
                dve.wait_ge(hid_hi_made, it * HIDDEN + u + 1)
                dve.tensor_tensor(hid_lo[:, u % HID_SLOTS, :], hid[:, u % 2, :],
                                  hid_hi[:, u % HID_SLOTS, :].bitcast(F32), ALU.subtract).then_inc(hid_lo_made, 1)

            def slot_free(it, u):
                half, f = divmod(u, FT)
                if f == FT - 1:
                    return fc2_full, it * 4 + 2 * half + 2
                return hid_used, it * (HIDDEN - 2) + u - half + 1

            def attention(it, layer):
                for step in range(LAST_STEP + 1):
                    if layer == 1 and step in SUM_AT:
                        sum_rotated(it, SUM_AT[step])
                    for s, g in quad_at(step, 0):
                        row_max(it, s, g)
                    for s, b in batch_at(step, AT_Z):
                        normalise(it, s + 1, b)
                    if layer == 0 and step == AT_MASK:
                        dve.wait_ge(side_loaded, (it + 1) * 32)
                        dve.tensor_scalar(mask_row[:], mask_u8[:], MASKED / P, None, ALU.mult).then_inc(mask_made, 1)
                    for s, g in quad_at(step, AT_TURN):
                        move_probs(it, s, g)
                    for s, b in batch_at(step, AT_RDEN):
                        make_rden(it, s, b)
                    for s, b in batch_at(step, AT_SCALE):
                        scale_heads(it, s, b)
                    for s, b in batch_at(step, AT_PROJ):
                        take_output(it, layer, 4 * s + b)
                    for s, b in batch_at(step, AT_STATS):
                        moments(it, layer, s + 1, b)
                    if step in SIDE:
                        move_side(it, layer, step)
                    if layer == 1:
                        for unit in roped_at(step, SWAP_LAG):
                            swap(it, unit)
                            if unit[0] == "q":
                                times_sin(it, unit)
                        if step in MASK_AT:
                            high_keys(it, layer, MASK_AT[step])
                    for kind, u in FIRST_HALF.get(step, ()):
                        if kind == "up":
                            split_hidden(it, u)

            dve.memset(ones_row[:], 1.0).then_inc(ready, 1)
            for s in range(2):
                dve.memset(v_pad[s][:], 0.0).then_inc(ready, 1)
            dve.memset(mod[:, 5:7, 0:B], 1.0).then_inc(ready, 1)
            dve.memset(mod[:, 7:9, 0:B], 0.0).then_inc(ready, 1)
            dve.memset(mod[:, :, LAYERS * B:], 1.0).then_inc(ready, 1)
            for layer in range(LAYERS):
                dve.memset(eps_cols[:, layer:layer + 1], EPS[layer]).then_inc(ready, 1)
                dve.memset(mod[:, 4, layer * B:(layer + 1) * B], EPS[layer]).then_inc(ready, 1)
            dve.wait_ge(silu_step, 1)
            dve.tensor_scalar(silu_tmp[:], silu_tmp[:], 1.0, None, ALU.add).then_inc(silu_step, 1)
            dve.wait_ge(silu_step, 2)
            dve.reciprocal(silu_tmp[:], silu_tmp[:]).then_inc(silu_step, 1)
            dve.wait_ge(silu_step, 3)
            dve.tensor_tensor(silu[:], cond[:], silu_tmp[:], ALU.mult).then_inc(silu_step, 1)
            dve.tensor_scalar(bias_cols[:, 4:8], bias_cols[:, 4:8], SCALE, None, ALU.mult).then_inc(ready, 1)
            dve.wait_ge(mod_full, 1)
            def put_mod(layer, k, src, bias):
                row = 0 if k == 0 else 1 + 4 * k
                dve.tensor_tensor(mod[:, row:row + 4, layer * B:(layer + 1) * B],
                                  src.rearrange("p (m b) -> p m b", m=4),
                                  bias.unsqueeze(2).broadcast_to([P, 4, B]), ALU.add).then_inc(mod_step, 1)

            for m, k in enumerate((0, 2)):
                put_mod(0, k, mix[:, m * 4 * B:(m + 1) * 4 * B], bias_mod[:, 4 * m:4 * m + 4])
            dve.tensor_tensor(raw[0:B, 1, :], p_proj[0:B, :],
                              raw[0:B, 0, :], ALU.add).then_inc(y_moved, 1)
            dve.wait_ge(mod_full, 2)
            for k in range(3):
                put_mod(1, k, score_banks[2][:, k * 4 * B:(k + 1) * 4 * B], bias_mod[:, 8 + 4 * k:12 + 4 * k])
            dve.wait_ge(mod_step, 5)
            for layer, k in ((0, 0), (0, 2), (1, 0), (1, 1), (1, 2)):
                row = 0 if k == 0 else 1 + 4 * k
                scales = mod[:, row:row + 2, layer * B:(layer + 1) * B]
                dve.tensor_scalar(scales, scales, 1.0, None, ALU.add).then_inc(mod_step, 1)
            dve.wait_ge(mod_step, 10)
            dve.wait_ge(ready, 11)
            dve.tensor_copy(mod_first[:], mod[:, 0:5, 0:GB]).then_inc(first_copied, 1)
            for b in range(GB):
                moments(0, 0, 0, b)
            for b in range(GB):
                normalise(0, 0, b)

            tail = ("m0 m1 z0 z1 h8 o8 h9 o9 m2 h10 m3 h11 z2 z3 h12 h13 h14 h15 o10 o11").split()
            for layer in range(LAYERS):
                for c in range(4):
                    n = 4 * layer + c
                    dve.wait_ge(w_hi_made, n + 1)
                    dve.tensor_tensor(w_lo[:, c * CHUNK:(c + 1) * CHUNK], stage[:, (c % 2) * CHUNK:(c % 2 + 1) * CHUNK],
                                      w_hi[:, c * CHUNK:(c + 1) * CHUNK].bitcast(F32), ALU.subtract).then_inc(w_lo_made, 1)
                with dve.Fori(0, NG) as i:
                    it = i + layer * NG
                    dve.tensor_copy(mod_now[:], mod[:, 5:13, bass.ds(i * GB + layer * B, GB)]).then_inc(mod_copied, 1)
                    if layer == 0:
                        for n in range(len(FIRST)):
                            move_first(it, n)
                    else:
                        keys, queries = ROPED[0:2]
                        swap(it, keys)
                        times_sin(it, keys)
                        swap(it, queries)
                        sum_rotated(it, keys)
                        times_sin(it, queries)
                        sum_rotated(it, queries)
                        high_keys(it, layer, keys)
                    attention(it, layer)
                    dve.tensor_copy(mod_first[:], mod[:, 0:5, bass.ds(i * GB + (layer * B + GB), GB)])\
                       .then_inc(first_copied, 1)
                    for what in tail:
                        n = int(what[1:])
                        if what[0] == "h":
                            split_hidden(it, n)
                        elif what[0] == "o":
                            take_output(it, layer, n)
                        elif what[0] == "m":
                            moments(it + 1, layer, 0, n)
                        else:
                            normalise(it + 1, 0, n)

        @block.gpsimd
        def _(pool):
            def make_rstd(it, layer, k, b):
                j = 4 * k + b
                pool.wait_ge(moments_made, it * 12 + j + 1)
                if k == 0 and b == 0:
                    pool.wait_ge(first_copied, it + 1)
                eps = mod_first[:, 4, 0:1] if k == 0 else eps_cols[:, layer:layer + 1]
                pool.tensor_tensor(var_eps[:, b:b + 1], mean_var[:, b, 1:2], eps, ALU.add).then_inc(eps_added, 1)
                pool.wait_ge(eps_added, it * 12 + j + 1)
                pool.tensor_tensor(rstd[:, b:b + 1], var_eps[:, b:b + 1], minus_half[:], ALU.pow).then_inc(rstd_made, 1)

            def split_xt(it, k, b):
                pool.wait_ge(xt_hi_made, it * 12 + 4 * k + b + 1)
                cols = slice(b * N, (b + 1) * N)
                pool.tensor_tensor(xt_lo[:, :, cols], xt[:, b % 2], xt_hi[:, :, cols].bitcast(F32), ALU.subtract)\
                    .then_inc(xt_lo_made, 1)

            def add_output(it, layer, j):
                b = j % 4
                if layer == 1 and j < 8:
                    return
                y_out(pool, it, j)
                if layer == 0 and not 4 <= j < 8:
                    g = j // 8
                    if j == 0:
                        pool.wait_ge(side_loaded, (it + 1) * 32)
                    pool.tensor_tensor(delta[:, j % 2, :], delta[:, j % 2, :], gate_now[:, b, g, :], ALU.mult)\
                        .then_inc(gated, 1)
                    pool.wait_ge(gated, it * 8 + (j if j < 4 else j - 4) + 1)
                if j == 0:
                    pool.wait_ge(stored, it * 16 + 16 * GATE_STORES)
                pool.tensor_tensor(x[:, b, :], x_new[:, b, :] if j < 4 else x[:, b, :], delta[:, j % 2, :], ALU.add)\
                    .then_inc(x_updated, 1)

            def times_cos(it, unit):
                n, which = ROPED.index(unit), int(unit[0] == "q")
                pool.wait_ge(swapped, (it - NG) * len(ROPED) + n + 1)
                blocks = lambda v: v[:, which, :].rearrange("p (b n) -> p b n", b=GB)
                pool.tensor_tensor(blocks(raw), blocks(raw), cos_t[:].unsqueeze(1).broadcast_to([P, GB, N]), ALU.mult)\
                    .then_inc(cos_made, 1)

            def finish_keys(it, unit):
                kind, s, half = unit
                g, n = it - NG, ROPED.index(unit)
                rot3 = rot[:, 0, :].rearrange("p (b n) -> p b n", b=GB)
                pool.tensor_tensor(rot3, rot3, sin_t[:].unsqueeze(1).broadcast_to([P, GB, N]), ALU.mult)\
                    .then_inc(sin_keys, 1)
                pool.wait_ge(cos_made, g * len(ROPED) + n + 1)
                pool.wait_ge(sin_keys, g * 3 + 2 * s + half)
                pool.tensor_tensor(rot[:, 0, :], raw[:, 0, :], rot[:, 0, :], ALU.add).then_inc(keys_summed, 1)

            def attention(it, layer):
                for step in range(LAST_STEP + 1):
                    for s, b in batch_at(step, AT_PROJ):
                        add_output(it, layer, 4 * s + b)
                    for s, b in batch_at(step, AT_STATS):
                        make_rstd(it, layer, s + 1, b)
                    for s, b in batch_at(step, AT_LNT):
                        split_xt(it, s + 1, b)
                    for unit in roped_at(step, SWAP_LAG) if layer == 1 else ():
                        times_cos(it, unit)
                        if unit[0] == "k":
                            finish_keys(it, unit)
                    if step == AT_CTX:
                        pool.wait_ge(ctx_hi_made, it + 1)
                        pool.tensor_tensor(ctx_lo[:], ctxt[:], ctx_hi[:].bitcast(F32), ALU.subtract).then_inc(ctx_lo_made, 1)

            pool.memset(minus_half[:], -0.5).then_inc(half_made, 1)
            pool.wait_ge(half_made, 1)
            for b in range(GB):
                make_rstd(0, 0, 0, b)
            for b in range(GB):
                split_xt(0, 0, b)
            tail = ("r0 r1 r2 x0 r3 x1 o8 o9 x2 x3 o10 o11").split()
            for layer in range(LAYERS):
                with pool.Fori(0, NG) as i:
                    it = i + layer * NG
                    if layer == 1:
                        times_cos(it, ROPED[0])
                        times_cos(it, ROPED[1])
                    attention(it, layer)
                    for what in tail:
                        n = int(what[1:])
                        if what[0] == "o":
                            add_output(it, layer, n)
                        elif what[0] == "r":
                            make_rstd(it + 1, layer, 0, n)
                        else:
                            split_xt(it + 1, 0, n)


SWAP = [16 * (p // 16) + (p % 16 + HD // 2) % HD for p in range(32)]

WEIGHTS = [
    [[("L0_xcond_qkv_w", W_QKV, CT, 3 * D), ("L0_xcond_sa_proj_w", W_SA, CT, D)],
     [("L0_xcond_q_w", W_Q, CT, D), ("L0_xcond_kv_w", W_KV, CT, 2 * D), ("L0_xcond_ca_proj_w", W_CA, CT, D)],
     [("L0_xcond_fc1_w", W_F1, CT, DF)],
     [("L0_xcond_fc2_w", W_F2, FT, D)]],
    [[("L1_qkv_wT", W_QKV, CT, 3 * D), ("L1_sa_wT", W_SA, CT, D)],
     [("L1_q_wT", W_Q, CT, D), ("L1_kv_wT", W_KV, CT, 2 * D), ("L1_ca_wT", W_CA, CT, D)],
     [("L1_f1_wT", W_F1, CT, DF)],
     [("L1_f2_wT", W_F2, FT, D)]],
]
_PARTS = [len(c) for layer in WEIGHTS for c in layer]
W_LOADS = [sum(_PARTS[n % 2:n + 1:2]) for n in range(len(_PARTS))]


def rope_tables():
    half = HD // 2
    inv = (1.0 / np.float32(10000.0) ** (np.arange(half, dtype=np.float32) / np.float32(half))).astype(np.float32)
    ang = np.arange(N, dtype=np.float32)[None, :] * inv[:, None]
    cos, sin = np.cos(ang), np.sin(ang)
    return np.tile(cos, (P // half, 1)), np.tile(np.concatenate([-sin, sin]), (P // HD, 1))


def kernel(**inputs):
    import concourse.bacc as bacc
    from concourse.bass_utils import run_bass_kernel_spmd as run

    get = {k: np.asarray(v) for k, v in inputs.items()}
    cols = lambda v: v.reshape(-1, P).T
    zeros = np.zeros
    ada_b = get["L0_xcond_ada_b"].reshape(6, D)
    qkv_b = get["L0_xcond_qkv_b"].reshape(3, D)
    kv_b = get["L0_xcond_kv_b"].reshape(2, D)
    cos, sin = rope_tables()
    arrays = {
        "x": get["x"].reshape(B * N, D),
        "condT": get["cond_1024"].T,
        "ctxT": get["ctx_1024"].reshape(B * N, D).T,
        "mask": get["mask_BxS2_bf0"].reshape(B * N).view(np.uint32),
        "L0_xcond_ada_w": get["L0_xcond_ada_w"],
        "ln_wT": np.stack([get[f"L1_xcond_ln{k}_w"].T for k in (1, 2, 3)]),
        "bias_mod": np.concatenate([cols(ada_b[c]) for c in (1, 0, 4, 3)]
                                   + [cols(get[f"L1_xcond_ln{k}_b"]) for k in (1, 2, 3)], axis=1),
        "gate_bias": np.stack([ada_b[2], ada_b[5]]),
        "ident": np.eye(P, dtype=np.float32),
        "head_mask": (np.arange(P)[:, None] % (COPIES * HD) // HD == np.arange(COPIES)).astype(np.float32),
        "cos_t": cos,
        "sin_t": sin,
        "bias_rows": np.stack([qkv_b[2], kv_b[1], get["L0_xcond_sa_proj_b"], get["L0_xcond_ca_proj_b"],
                               get["L0_xcond_fc2_b"], get["L1_xcond_ffn_b2"]]),
        "bias_cols": np.concatenate([cols(qkv_b[1]), cols(kv_b[0]), cols(qkv_b[0]), cols(get["L0_xcond_q_b"]),
                                     cols(get["L0_xcond_fc1_b"]), cols(get["L1_xcond_ffn_b1"])], axis=1),
        "L1_qkv_wT": get["L1_xcond_qkv_w"].T,
        "L1_sa_wT": get["L1_xcond_sa_out_w"].T,
        "L1_q_wT": get["L1_xcond_q_w"].T,
        "L1_kv_wT": np.concatenate([get["L1_xcond_k_w"].T, get["L1_xcond_v_w"].T], axis=1),
        "L1_ca_wT": get["L1_xcond_ca_out_w"].T,
        "L1_f1_wT": get["L1_xcond_ffn_w1"].T,
        "L1_f2_wT": get["L1_xcond_ffn_w2"].T,
    }
    for name in ("qkv", "sa_proj", "q", "kv", "ca_proj", "fc1", "fc2"):
        arrays[f"L0_xcond_{name}_w"] = get[f"L0_xcond_{name}_w"]
    arrays = {k: np.ascontiguousarray(v) for k, v in arrays.items()}

    nc = bacc.Bacc("TRN2", target_bir_lowering=False, num_devices=1)
    a = {k: nc.dram_tensor(f"in_{k}", v.shape, mybir.dt.from_np(v.dtype), kind="ExternalInput").ap()
         for k, v in arrays.items()}
    x_mid = nc.dram_tensor("x_mid", (B * N, D), F32, kind="Internal").ap()
    gates = nc.dram_tensor("gates", (B, 2, D), F32, kind="Internal").ap()
    out = nc.dram_tensor("out", (B * N, D), F32, kind="ExternalOutput").ap()
    build_blocks(nc, a, x_mid, gates, out)
    r = run(nc, [{f"in_{k}": v for k, v in arrays.items()}], core_ids=[0])
    return r.results[0]["out"].reshape(B, N, D)
```
